# Optimizing a Trainium2 kernel written in Bass

```python
import numpy as np
import jax
import jax.numpy as jnp

def _softmax(x, axis=-1):
    return jax.nn.softmax(x, axis=axis)
def _gelu(x):
    return jax.nn.gelu(x, approximate=True)
def _silu(x):
    return jax.nn.silu(x)
def _sigmoid(x):
    return jax.nn.sigmoid(x)
def _layernorm(x, axis=-1, eps=1e-5):
    m = jnp.mean(x, axis=axis, keepdims=True)
    v = jnp.var(x, axis=axis, keepdims=True)
    return (x - m) / jnp.sqrt(v + eps)
def _scatter_add(tgt, idx, src, axis=0):
    return tgt.at[idx].add(src)
def _segment_sum(src, seg, n):
    return jax.ops.segment_sum(src, seg, n)

kernel_name = 'mk_conv_attn_hybrid_d2_conv_nchw256_63e40d'

def setup_inputs(seed: int = 0):
    np.random.seed(seed)
    _w = jnp.asarray
    def _rec_inputs():
        import jax
        import jax.numpy as jnp
        _gk = jax.random.key(seed)
        x = -0.0005207 + 1.001 * jax.random.normal(jax.random.fold_in(_gk, 1), (2, 256, 64, 64), jnp.float32)
        return x
    x = _rec_inputs()
    def _L0_conv_setup():
        import jax, jax.numpy as jnp
        import numpy as np
        DIM = 256
        D_STATE = 16
        D_CONV = 4
        EXPAND = 2
        D_INNER = EXPAND * DIM
        DT_RANK = (DIM + 15) // 16
        B_SZ, H_SZ, W_SZ = (2, 64, 64)

        def silu(u):
            return u * jax.nn.sigmoid(u)
        key = jax.random.key(seed)
        ks = jax.random.split(key, 8)
        s = 0.02
        return {'x': jax.random.normal(ks[0], (B_SZ, DIM, H_SZ, W_SZ), dtype=jnp.float32), 'ln_g': jnp.ones((DIM,), jnp.float32), 'ln_b': jnp.zeros((DIM,), jnp.float32), 'W_in': jax.random.normal(ks[1], (DIM, 2 * D_INNER), dtype=jnp.float32) * s, 'conv_w': jax.random.normal(ks[2], (D_INNER, 1, D_CONV), dtype=jnp.float32) * s, 'conv_b': jnp.zeros((D_INNER,), jnp.float32), 'W_x': jax.random.normal(ks[3], (D_INNER, DT_RANK + 2 * D_STATE), dtype=jnp.float32) * s, 'W_dt': jax.random.normal(ks[4], (DT_RANK, D_INNER), dtype=jnp.float32) * s, 'b_dt': jnp.full((D_INNER,), -4.6, jnp.float32), 'A_log': jnp.log(jnp.broadcast_to(jnp.arange(1, D_STATE + 1, dtype=jnp.float32), (D_INNER, D_STATE))), 'D_skip': jnp.ones((D_INNER,), jnp.float32), 'W_out': jax.random.normal(ks[5], (D_INNER, DIM), dtype=jnp.float32) * s}
    _L0_conv_all = _L0_conv_setup()
    _L0_conv_in = {k: v for k, v in _L0_conv_all.items() if k in ('ln_g', 'ln_b', 'W_in', 'conv_w', 'conv_b', 'W_x', 'W_dt', 'b_dt', 'A_log', 'D_skip', 'W_out', )}
    del _L0_conv_all

    def _L1_attn_setup():
        import jax, jax.numpy as jnp
        import numpy as np
        NUM_HEADS = 8
        DIM = 256
        key = jax.random.key(seed)
        k1, k2, k3, k4 = jax.random.split(key, 4)
        B, N, C = (2, 4096, DIM)
        x = jax.random.normal(k1, (B, N, C), dtype=jnp.float32)
        w_qkv = jax.random.normal(k2, (3 * C, C), dtype=jnp.float32) * C ** (-0.5)
        w_proj = jax.random.normal(k3, (C, C), dtype=jnp.float32) * C ** (-0.5)
        b_proj = jax.random.normal(k4, (C,), dtype=jnp.float32) * 0.01
        temperature = jnp.ones((1,), dtype=jnp.float32)
        return {'x': x, 'w_qkv': w_qkv, 'w_proj': w_proj, 'b_proj': b_proj, 'temperature': temperature}
    _L1_attn_all = _L1_attn_setup()
    _L1_attn_in = {k: v for k, v in _L1_attn_all.items() if k in ('w_qkv', 'w_proj', 'b_proj', 'temperature', )}
    del _L1_attn_all

    def _L1_ffn_setup():
        import jax, jax.numpy as jnp
        import numpy as np
        NUM_EXPERTS = 8
        TOP_K = 2
        B, S, D = (8, 8192, 256)

        def _moe(tokens, router_w, w1, b1, w2, b2):
            N = tokens.shape[0]
            E = router_w.shape[0]
            logits = tokens.astype(jnp.float32) @ router_w.astype(jnp.float32).T
            probs = jax.nn.softmax(logits, axis=-1)
            rw, re = jax.lax.top_k(probs, TOP_K)
            if TOP_K > 1:
                rw = rw / jnp.maximum(rw.sum(-1, keepdims=True), 1e-12)
            rw = rw.astype(tokens.dtype)
            combine = jnp.zeros((N, E), tokens.dtype).at[jnp.arange(N)[:, None], re].set(rw)
            out = tokens
            for e in range(E):
                h = jax.nn.gelu(tokens @ w1[e] + b1[e], approximate=False)
                y = h @ w2[e] + b2[e]
                out = out + combine[:, e:e + 1] * y
            return out
        key = jax.random.key(seed)
        ks = jax.random.split(key, 4)
        scale = 1.0 / np.sqrt(D).astype(np.float32)
        return {'input_embeddings': jax.random.normal(ks[0], (B, S, D), jnp.float32), 'router_w': jax.random.normal(ks[1], (NUM_EXPERTS, D), jnp.float32) * scale, 'w1': jax.random.normal(ks[2], (NUM_EXPERTS, D, D), jnp.float32) * scale, 'b1': jnp.zeros((NUM_EXPERTS, D), jnp.float32), 'w2': jax.random.normal(ks[3], (NUM_EXPERTS, D, D), jnp.float32) * scale, 'b2': jnp.zeros((NUM_EXPERTS, D), jnp.float32)}
    _L1_ffn_all = _L1_ffn_setup()
    _L1_ffn_in = {k: v for k, v in _L1_ffn_all.items() if k in ('router_w', 'w1', 'b1', 'w2', 'b2', )}
    del _L1_ffn_all

    return {
        "x": x,
        "L0_conv_ln_g": _L0_conv_in["ln_g"],
        "L0_conv_ln_b": _L0_conv_in["ln_b"],
        "L0_conv_W_in": _L0_conv_in["W_in"],
        "L0_conv_conv_w": _L0_conv_in["conv_w"],
        "L0_conv_conv_b": _L0_conv_in["conv_b"],
        "L0_conv_W_x": _L0_conv_in["W_x"],
        "L0_conv_W_dt": _L0_conv_in["W_dt"],
        "L0_conv_b_dt": _L0_conv_in["b_dt"],
        "L0_conv_A_log": _L0_conv_in["A_log"],
        "L0_conv_D_skip": _L0_conv_in["D_skip"],
        "L0_conv_W_out": _L0_conv_in["W_out"],
        "L1_attn_w_qkv": _L1_attn_in["w_qkv"],
        "L1_attn_w_proj": _L1_attn_in["w_proj"],
        "L1_attn_b_proj": _L1_attn_in["b_proj"],
        "L1_attn_temperature": _L1_attn_in["temperature"],
        "L1_ffn_router_w": _L1_ffn_in["router_w"],
        "L1_ffn_w1": _L1_ffn_in["w1"],
        "L1_ffn_b1": _L1_ffn_in["b1"],
        "L1_ffn_w2": _L1_ffn_in["w2"],
        "L1_ffn_b2": _L1_ffn_in["b2"],
    }

def reference(x, L0_conv_ln_g, L0_conv_ln_b, L0_conv_W_in, L0_conv_conv_w, L0_conv_conv_b, L0_conv_W_x, L0_conv_W_dt, L0_conv_b_dt, L0_conv_A_log, L0_conv_D_skip, L0_conv_W_out, L1_attn_w_qkv, L1_attn_w_proj, L1_attn_b_proj, L1_attn_temperature, L1_ffn_router_w, L1_ffn_w1, L1_ffn_b1, L1_ffn_w2, L1_ffn_b2):
    import jax
    import jax.numpy as jnp
    def _L0_conv_ref(x, ln_g, ln_b, W_in, conv_w, conv_b, W_x, W_dt, b_dt, A_log, D_skip, W_out):
        import jax, jax.numpy as jnp
        import numpy as np
        DIM = 256
        D_STATE = 16
        D_CONV = 4
        EXPAND = 2
        D_INNER = EXPAND * DIM
        DT_RANK = (DIM + 15) // 16
        B_SZ, H_SZ, W_SZ = (2, 64, 64)

        def silu(u):
            return u * jax.nn.sigmoid(u)
        B, C, H, W = x.shape
        L = H * W
        xs = x.reshape(B, C, L).transpose(0, 2, 1)
        mu = jnp.mean(xs, axis=-1, keepdims=True)
        var = jnp.mean((xs - mu) ** 2, axis=-1, keepdims=True)
        xs = (xs - mu) / jnp.sqrt(var + 1e-05) * ln_g + ln_b
        xz = xs @ W_in
        xin, z = jnp.split(xz, 2, axis=-1)
        xc = xin.transpose(0, 2, 1)
        xc = jax.lax.conv_general_dilated(xc, conv_w, window_strides=(1,), padding=[(D_CONV - 1, 0)], dimension_numbers=('NCH', 'OIH', 'NCH'), feature_group_count=D_INNER)
        xc = silu(xc + conv_b[None, :, None])
        xin = xc.transpose(0, 2, 1)
        dbl = xin @ W_x
        dt = jax.nn.softplus(dbl[..., :DT_RANK] @ W_dt + b_dt)
        Bm = dbl[..., DT_RANK:DT_RANK + D_STATE]
        Cm = dbl[..., DT_RANK + D_STATE:]
        A = -jnp.exp(A_log)

        def step(h, inp):
            dt_t, b_t, c_t, x_t = inp
            dA = jnp.exp(dt_t[:, :, None] * A)
            h = dA * h + dt_t[:, :, None] * b_t[:, None, :] * x_t[:, :, None]
            y = jnp.einsum('bdn,bn->bd', h, c_t)
            return (h, y)
        h0 = jnp.zeros((B, D_INNER, D_STATE), xin.dtype)
        seq = (dt.transpose(1, 0, 2), Bm.transpose(1, 0, 2), Cm.transpose(1, 0, 2), xin.transpose(1, 0, 2))
        _, ys = jax.lax.scan(step, h0, seq)
        y = ys.transpose(1, 0, 2) + xin * D_skip
        y = y * silu(z)
        out = y @ W_out
        return out.transpose(0, 2, 1).reshape(B, C, H, W)

    def _L1_attn_ref(x, w_qkv, w_proj, b_proj, temperature):
        import jax, jax.numpy as jnp
        import numpy as np
        NUM_HEADS = 8
        DIM = 256
        B, N, C = x.shape
        H = NUM_HEADS
        d = C // H
        scale = C ** (-0.5)
        qkv = (x @ w_qkv.T).reshape(B, N, 3, H, d).transpose(2, 0, 3, 1, 4)
        q, k, v = (qkv[0], qkv[1], qkv[2])
        attn = jnp.einsum('bhnd,bhmd->bhnm', q, k) * scale
        diag_mask = jnp.eye(N, dtype=attn.dtype) * jnp.asarray(-1000000000.0, attn.dtype)
        attn = attn - diag_mask
        attn = jax.nn.softmax(attn / temperature[0], axis=-1)
        out = jnp.einsum('bhnm,bhmd->bhnd', attn, v)
        out = out.transpose(0, 2, 1, 3).reshape(B, N, C)
        return out @ w_proj.T + b_proj

    def _L1_ffn_ref(input_embeddings, router_w, w1, b1, w2, b2):
        import jax, jax.numpy as jnp
        import numpy as np
        NUM_EXPERTS = 8
        TOP_K = 2
        B, S, D = (8, 8192, 256)

        def _moe(tokens, router_w, w1, b1, w2, b2):
            N = tokens.shape[0]
            E = router_w.shape[0]
            logits = tokens.astype(jnp.float32) @ router_w.astype(jnp.float32).T
            probs = jax.nn.softmax(logits, axis=-1)
            rw, re = jax.lax.top_k(probs, TOP_K)
            if TOP_K > 1:
                rw = rw / jnp.maximum(rw.sum(-1, keepdims=True), 1e-12)
            rw = rw.astype(tokens.dtype)
            combine = jnp.zeros((N, E), tokens.dtype).at[jnp.arange(N)[:, None], re].set(rw)
            out = tokens
            for e in range(E):
                h = jax.nn.gelu(tokens @ w1[e] + b1[e], approximate=False)
                y = h @ w2[e] + b2[e]
                out = out + combine[:, e:e + 1] * y
            return out
        b, s, d = input_embeddings.shape
        tokens = input_embeddings.reshape(b * s, d)
        return _moe(tokens, router_w, w1, b1, w2, b2).reshape(b, s, d)

    def _gn(v, G=32, eps=1e-5):
        B_, C_, H_, W_ = v.shape
        g = v.reshape(B_, G, C_ // G, H_, W_)
        m = jnp.mean(g, axis=(2, 3, 4), keepdims=True)
        s = jnp.var(g, axis=(2, 3, 4), keepdims=True)
        return ((g - m) / jnp.sqrt(s + eps)).reshape(v.shape)

    def _ln_c(v, eps=1e-6):
        m = jnp.mean(v, axis=1, keepdims=True)
        s = jnp.var(v, axis=1, keepdims=True)
        return (v - m) / jnp.sqrt(s + eps)

    def _ln_t(v, eps=1e-5):
        m = jnp.mean(v, axis=-1, keepdims=True)
        s = jnp.var(v, axis=-1, keepdims=True)
        return (v - m) / jnp.sqrt(s + eps)

    def _to_tokens(v):
        B_, C_, H_, W_ = v.shape
        return v.reshape(B_, C_, H_ * W_).transpose(0, 2, 1)
    def _from_tokens(t, like):
        B_, C_, H_, W_ = like.shape
        return t.transpose(0, 2, 1).reshape(B_, C_, H_, W_)

    x = x + _L0_conv_ref(_gn(x), L0_conv_ln_g, L0_conv_ln_b, L0_conv_W_in, L0_conv_conv_w, L0_conv_conv_b, L0_conv_W_x, L0_conv_W_dt, L0_conv_b_dt, L0_conv_A_log, L0_conv_D_skip, L0_conv_W_out)
    t = _to_tokens(x)
    t = t + _L1_attn_ref(_ln_t(t), L1_attn_w_qkv, L1_attn_w_proj, L1_attn_b_proj, L1_attn_temperature)
    t = t + _L1_ffn_ref(_ln_t(t), L1_ffn_router_w, L1_ffn_w1, L1_ffn_b1, L1_ffn_w2, L1_ffn_b2)
    x = _from_tokens(t, x)
    return x


_drawn_inputs = setup_inputs


def setup_inputs(seed=0):
    import zlib

    import numpy as np

    out = dict(_drawn_inputs(seed))
    spreads = {'L0_conv_ln_g': (1.0, 0.6),
     'L0_conv_ln_b': (0.0, 0.8),
     'L0_conv_conv_b': (0.0, 0.646),
     'L0_conv_b_dt': (-4.599999904632568, 0.6),
     'L0_conv_D_skip': (1.0, 0.6),
     'L1_ffn_b1': (0.0, 2.0),
     'L1_ffn_b2': (0.0, 0.8)}
    factors = {'L0_conv_W_in': 5.722,
     'L0_conv_conv_w': 8.0,
     'L0_conv_W_x': 8.0,
     'L0_conv_W_dt': 8.0,
     'L0_conv_A_log': 8.0,
     'L0_conv_W_out': 5.388,
     'L1_attn_b_proj': 37.0}
    for name, (base, spread) in spreads.items():
        noise = np.random.default_rng([zlib.crc32(name.encode()), seed]).standard_normal(out[name].shape)
        drawn = base * np.exp(spread * noise) if base else spread * noise
        out[name] = jnp.asarray(drawn.astype(out[name].dtype))
    for name, factor in factors.items():
        out[name] = (out[name] * factor).astype(out[name].dtype)
    return out
```

```python
from contextlib import ExitStack

import numpy as np

import concourse.bass as bass
from concourse import mybir

ALU = mybir.AluOpType
ACT = mybir.ActivationFunctionType
AX = mybir.AxisListType
F32 = mybir.dt.float32
F16 = mybir.dt.float16
BF16 = mybir.dt.bfloat16
U32 = mybir.dt.uint32
RMAX = bass.bass_isa.ReduceOp.max

P = 128
B = 2
C = 256
L = 4096
KT = C // P
T = 512
CPB = L // T
NCH = B * CPB
DI = 512
MT = DI // P
NS = 16
DTR = 16
TAPS = 4
LAG = 2
SLOTS = 4
H = 8
HD = C // H
HP = H // 2
E_ = 8
LN_EPS = 1e-5
GN_EPS = 1e-5


def ds1(i):
    return bass.ds(i, 1)


def chunk_view(t, c):
    return t[ds1(c)].rearrange("o p k t -> (o p) k t")


def group_norm_stats(nc, sems, ctx, x, gn_mean, scale_of, shift_of):
    def sb(name, shape, dt=F32):
        return ctx.enter_context(nc.sbuf_tensor(name, shape, dt))

    xs = sb("gn_x", [P, NCH, KT, T])
    blk = sb("gn_blk", [P, P])
    stats = sb("gn_stats", [P, B * KT, CPB, 6])
    mv = sb("gn_mv", [P, B * KT, 2])
    means = sb("gn_means", [P, B * KT])
    dev = sb("gn_dev", [P, B * KT])
    spread = sb("gn_spread", [P, B * KT])
    gmean = sb("gn_gmean", [P, B * KT])
    lnv = sb("gn_lnv", [P, B * KT])
    rstd = sb("gn_rstd", [P, B * KT])
    shift = sb("gn_shift", [P, B * KT])
    epsc = sb("gn_eps", [P, 1])
    ps = ctx.enter_context(nc.psum_tensor("gn_ps", [P, 2, T], F32))
    loaded = [sems.enter_context(nc.semaphore(f"gn_loaded{b}")) for b in range(B)]
    blk_loaded = sems.enter_context(nc.semaphore("gn_blk_loaded"))
    steps = sems.enter_context(nc.semaphore("gn_vector_steps"))
    group_mean = sems.enter_context(nc.semaphore("gn_group_mean"))
    rstd_ready = sems.enter_context(nc.semaphore("gn_rstd_ready"))

    with nc.Block() as block:
        @block.sync
        def _(sp):
            for b in range(B):
                for c in range(b * CPB, (b + 1) * CPB):
                    sp.dma_start(xs[:, c], x[c]).then_inc(loaded[b], 16)
            sp.dma_start(blk[:], gn_mean).then_inc(blk_loaded, 16)

        @block.vector
        def _(dve):
            v = nc.vector
            done = [0]

            def step(ins):
                done[0] += 1
                ins.then_inc(steps, 1)
                dve.wait_ge(steps, done[0])

            step(v.memset(epsc[:], GN_EPS))
            for b in range(B):
                dve.wait_ge(loaded[b], 16 * CPB)
                for c in range(CPB):
                    for k in range(KT):
                        ins = v.bn_stats(stats[:, b * KT + k, c], xs[:, b * CPB + c, k])
            step(ins)
            for q in range(B * KT):
                ins = v.bn_aggr(mv[:, q], stats[:, q].rearrange("p c s -> p (c s)"))
            step(ins)
            step(v.tensor_copy(means[:], mv[:, :, 0]))
            dve.wait_ge(group_mean, 1)
            step(v.tensor_copy(gmean[:], ps[:, 0, 0:B * KT]))
            step(v.tensor_tensor(dev[:], mv[:, :, 0], gmean[:], ALU.subtract))
            step(v.tensor_tensor(dev[:], dev[:], dev[:], ALU.mult))
            step(v.tensor_tensor(spread[:], dev[:], mv[:, :, 1], ALU.add))
            dve.wait_ge(rstd_ready, 2)
            step(v.scalar_tensor_tensor(out=shift[:], in0=gmean[:], scalar=-1.0, in1=rstd[:],
                                        op0=ALU.mult, op1=ALU.mult))
            for c in range(NCH):
                q = (c // CPB) * KT
                v.tensor_copy(scale_of[:, c], rstd[:, q:q + KT])
                ins = v.tensor_copy(shift_of[:, c], shift[:, q:q + KT])
            step(ins)

        @block.tensor
        def _(pe):
            pe.wait_ge(blk_loaded, 16)
            pe.wait_ge(steps, 4)
            nc.tensor.matmul(ps[:, 0, 0:B * KT], blk[:], means[:], start=True, stop=True).then_inc(group_mean, 1)
            pe.wait_ge(steps, 8)
            nc.tensor.matmul(ps[:, 1, 0:B * KT], blk[:], spread[:], start=True, stop=True).then_inc(group_mean, 1)

        @block.scalar
        def _(act):
            act.wait_ge(group_mean, 2)
            nc.scalar.activation(lnv[:], ps[:, 1, 0:B * KT], ACT.Ln, bias=epsc[:, 0:1]).then_inc(rstd_ready, 1)
            act.wait_ge(rstd_ready, 1)
            nc.scalar.activation(rstd[:], lnv[:], ACT.Exp, scale=-0.5).then_inc(rstd_ready, 1)


def state_space_layer(nc, sems, ctx, x, w, scale_of, shift_of, x1):
    def sb(name, shape, dt=F32):
        return ctx.enter_context(nc.sbuf_tensor("l0_" + name, shape, dt))

    def sem(name):
        return sems.enter_context(nc.semaphore("l0_" + name))

    ones = sb("ones", [P, P])
    ident = sb("ident", [P, P])
    w_in = sb("w_in", [P, KT, 2 * DI])
    w_x = sb("w_x", [P, MT, 2 * NS + DTR])
    w_dt = sb("w_dt", [DTR, DI])
    w_out = sb("w_out", [P, MT, C])
    select = sb("select", [3 * 2 * NS, 2 * NS, P], BF16)
    cols = sb("cols", [P, 2 * KT + MT * (TAPS + 3)])
    a_log = sb("a_log", [P, MT, NS])
    neg_a = sb("neg_a", [P, MT, NS])
    keep = sb("keep", [P, NCH + 1])
    epsc = sb("eps", [P, 2])
    ln_g = cols[:, 0:KT]
    ln_b = cols[:, KT:2 * KT]
    o = 2 * KT
    taps = cols[:, o:o + MT * TAPS].rearrange("p (m k) -> p m k", m=MT)
    conv_b = cols[:, o + MT * TAPS:o + MT * (TAPS + 1)]
    b_dt = cols[:, o + MT * (TAPS + 1):o + MT * (TAPS + 2)]
    d_skip = cols[:, o + MT * (TAPS + 2):o + MT * (TAPS + 3)]

    xb = sb("xb", [P, KT, T])
    xh = sb("xh", [P, KT, T])
    dn = sb("dn", [P, KT, T])
    sq = sb("sq", [P, KT, T])
    rs = sb("rs", [P, T])
    xi = sb("xi", [P, MT, T + TAPS - 1])
    cv = sb("cv", [P, MT, T])
    xc = [sb(f"xc{j}", [P, MT, T]) for j in range(2)]
    sz = [sb(f"sz{j}", [P, MT, T]) for j in range(2)]
    dt = [sb(f"dt{j}", [P, MT, T]) for j in range(2)]
    dtx = [sb(f"dtx{j}", [P, MT, T]) for j in range(2)]
    dlow = sb("dlow", [DTR, T])
    bcf = sb("bcf", [2 * NS, 2, T])
    bcr = sb("bcr", [2 * NS, T], BF16)
    bc3 = [sb(f"bc3_{j}", [3 * 2 * NS, T], BF16) for j in range(2)]
    dec = sb("dec", [P, 2, MT, T])
    st = sb("st", [P, SLOTS, MT, T])
    cb = sb("cb", [P, 2, T])
    last = sb("last", [P, NS, MT])
    xr = sb("xr", [P, KT, T])
    psy = ctx.enter_context(nc.psum_tensor("l0_psy", [P, MT, T], F32))
    psb = ctx.enter_context(nc.psum_tensor("l0_psb", [P, T], F32))
    psc = ctx.enter_context(nc.psum_tensor("l0_psc", [P, T], F32))
    psp = ctx.enter_context(nc.psum_tensor("l0_psp", [P, 2, T], F32))

    w_loaded = sem("w_loaded")
    set_up = sem("set_up")
    x_loaded = sem("x_loaded")
    xr_loaded = sem("xr_loaded")
    x1_stored = sem("x1_stored")
    xh_ready = sem("xh_ready")
    mean_ready = sem("mean_ready")
    d_ready = sem("d_ready")
    sq_ready = sem("sq_ready")
    var_ready = sem("var_ready")
    ln_ready = sem("ln_ready")
    rs_ready = sem("rs_ready")
    dn_ready = sem("dn_ready")
    xn_ready = sem("xn_ready")
    xz_ready = sem("xz_ready")
    xz_copied = sem("xz_copied")
    conv_first = sem("conv_first")
    conv_part = sem("conv_part")
    conv_ready = sem("conv_ready")
    bc_part = sem("bc_part")
    tail_kept = sem("tail_kept")
    sz_ready = sem("sz_ready")
    xc_ready = sem("xc_ready")
    bc_ready = sem("bc_ready")
    bc_split = sem("bc_split")
    dlow_copied = sem("dlow_copied")
    u_ready = sem("u_ready")
    u_copied = sem("u_copied")
    u_abs = sem("u_abs")
    sp_ready = sem("sp_ready")
    dt_ready = sem("dt_ready")
    dtx_ready = sem("dtx_ready")
    b_ready = sem("b_ready")
    c_ready = sem("c_ready")
    c_copied = sem("c_copied")
    dec_ready = sem("dec_ready")
    drive_ready = sem("drive_ready")
    states_ready = sem("states_ready")
    last_kept = sem("last_kept")
    hc_ready = sem("hc_ready")
    slot_free = sem("slot_free")
    y_skip = sem("y_skip")
    y_gated = sem("y_gated")
    out_ready = sem("out_ready")
    x1_ready = sem("x1_ready")

    WLOADS = [(ones[:], w["ones"]), (ident[:], w["ident"]), (w_in[:], w["W_in"]), (w_x[:], w["W_x"]),
              (w_dt[:], w["W_dt"]), (w_out[:], w["W_out"]), (select[:], w["select"]),
              (cols[:], w["cols"]), (a_log[:], w["A_log"])]

    XZ_PRODUCT = (4, 5, 6, 7)
    XZ_COPY = (5, 6, 7, 8)

    def pairs(eng, body):
        with eng.Fori(0, NCH // 2) as i:
            for j in range(2):
                body(i * 2 + j, j)

    with nc.Block() as block:
        @block.sync
        def _(sp):
            for dst, src in WLOADS:
                sp.dma_start(dst, src).then_inc(w_loaded, 16)

            def load_x(cn, src):
                if not isinstance(cn, int) or cn:
                    sp.wait_ge(xh_ready, KT * cn)
                sp.dma_start(xb[:], chunk_view(x, src)).then_inc(x_loaded, 16)

            def chunk(c, j):
                load_x(c + 1, (c + 1) % NCH)
                sp.wait_ge(x1_stored, 16 * c)
                sp.dma_start(xr[:], chunk_view(x, (c + NCH - 1) % NCH)).then_inc(xr_loaded, 16)
                sp.wait_ge(x1_ready, KT * (c + 1))
                sp.dma_start(chunk_view(x1, c), xr[:]).then_inc(x1_stored, 16)

            load_x(0, 0)
            pairs(sp, chunk)
            load_x(NCH + 1, 1)
            sp.wait_ge(x1_stored, 16 * NCH)
            sp.dma_start(xr[:], x[NCH - 1]).then_inc(xr_loaded, 16)
            sp.wait_ge(x1_ready, KT * (NCH + 1))
            sp.dma_start(x1[NCH], xr[:]).then_inc(x1_stored, 16)
            sp.wait_ge(x1_stored, 16 * (NCH + 1))

        @block.scalar
        def _(act):
            s = nc.scalar

            def norm_group(cn):
                act.wait_ge(x_loaded, 16 * (cn + 1))
                act.wait_ge(d_ready, KT * cn)
                for k in range(KT):
                    s.activation(xh[:, k], xb[:, k], ACT.Identity, scale=scale_of[:, ds1(cn % NCH), k:k + 1].rearrange("p o k -> p (o k)"),
                                 bias=shift_of[:, ds1(cn % NCH), k:k + 1].rearrange("p o k -> p (o k)")).then_inc(xh_ready, 1)

            def square(cn):
                act.wait_ge(d_ready, KT * (cn + 1))
                act.wait_ge(var_ready, cn)
                s.activation(sq[:], dn[:], ACT.Square).then_inc(sq_ready, 1)

            def rstd(cn):
                act.wait_ge(var_ready, cn + 1)
                act.wait_ge(dn_ready, KT * cn)
                s.activation(rs[:], psp[:, 1], ACT.Ln, bias=epsc[:, 0:1]).then_inc(ln_ready, 1)
                act.wait_ge(ln_ready, cn + 1)
                s.activation(rs[:], rs[:], ACT.Exp, scale=-0.5).then_inc(rs_ready, 1)

            def gain(cn):
                act.wait_ge(dn_ready, KT * (cn + 1))
                for k in range(KT):
                    s.activation(dn[:, k], dn[:, k], ACT.Identity, scale=ln_g[:, k:k + 1],
                                 bias=ln_b[:, k:k + 1]).then_inc(xn_ready, 1)

            def copy_xz(cn, jn, m):
                act.wait_ge(xz_ready, 2 * MT * cn + m + 1)
                if m == 0:
                    act.wait_ge(tail_kept, cn + 1)
                if m == MT:
                    act.wait_ge(y_gated, cn)
                dst = xi[:, m, TAPS - 1:] if m < MT else sz[jn][:, m - MT]
                s.activation(dst, psp[:, m % 2], ACT.Copy).then_inc(xz_copied, 1)

            def conv_tap0(cn):
                act.wait_ge(xz_copied, 2 * MT * cn + MT)
                act.wait_ge(dt_ready, cn)
                for m in range(MT):
                    s.activation(cv[:, m], xi[:, m, 0:T], ACT.Identity, scale=taps[:, m, 0:1],
                                 bias=conv_b[:, m:m + 1]).then_inc(conv_first, 1)

            def silus(cn, jn):
                act.wait_ge(xz_copied, 2 * MT * (cn + 1))
                s.activation(sz[jn][:], sz[jn][:], ACT.Silu).then_inc(sz_ready, 1)
                act.wait_ge(conv_ready, MT * (cn + 1))
                act.wait_ge(out_ready, KT * cn)
                s.activation(xc[jn][:], cv[:], ACT.Silu).then_inc(xc_ready, 1)

            def copy_u(cn, jn, m):
                act.wait_ge(u_ready, MT * cn + m + 1)
                if m == 0:
                    act.wait_ge(xc_ready, cn + 1)
                s.activation(cv[:, m], psp[:, m % 2], ACT.Abs, bias=b_dt[:, m:m + 1]).then_inc(u_abs, 1)
                s.activation(dt[jn][:, m], psp[:, m % 2], ACT.Identity, bias=b_dt[:, m:m + 1]).then_inc(u_copied, 1)

            def exp_part(cn):
                act.wait_ge(u_abs, MT * (cn + 1))
                s.activation(cv[:], cv[:], ACT.Exp, scale=-1.0).then_inc(sp_ready, 1)

            def log_part(cn):
                act.wait_ge(sp_ready, 2 * cn + 1)
                s.activation(cv[:], cv[:], ACT.Ln, bias=epsc[:, 1:2]).then_inc(sp_ready, 1)

            def decay(c, j, n):
                if n == 0:
                    act.wait_ge(dt_ready, c + 1)
                act.wait_ge(states_ready, MT * (NS * c + n + 1))
                for m in range(MT):
                    s.activation(dec[:, n % 2, m], dt[j][:, m], ACT.Exp, scale=neg_a[:, m, n:n + 1]).then_inc(dec_ready, 1)

            def copy_c(c, n):
                act.wait_ge(c_ready, NS * c + n + 1)
                act.wait_ge(hc_ready, NS * c + n + 1)
                s.activation(cb[:, n % 2], psc[:], ACT.Copy).then_inc(c_copied, 1)

            act.wait_ge(w_loaded, 16 * len(WLOADS))
            act.wait_ge(set_up, 4)
            s.activation(a_log[:], a_log[:], ACT.Exp).then_inc(set_up, 1)
            act.wait_ge(set_up, 5)
            s.activation(neg_a[:], a_log[:], ACT.Copy, scale=-1.0).then_inc(set_up, 1)
            act.wait_ge(set_up, 6)

            def prepare(n, cn, jn):
                if n == 2:
                    rstd(cn)
                if n == 3:
                    gain(cn)
                if n in XZ_COPY:
                    copy_xz(cn, jn, 2 * XZ_COPY.index(n))
                    copy_xz(cn, jn, 2 * XZ_COPY.index(n) + 1)
                if n == 6:
                    conv_tap0(cn)
                if n == 9:
                    silus(cn, jn)
                if n == 13:
                    norm_group(cn + 1)
                    copy_u(cn, jn, 0)
                    copy_u(cn, jn, 1)
                if n == 14:
                    copy_u(cn, jn, 2)
                    copy_u(cn, jn, 3)
                    exp_part(cn)
                if n == 15:
                    log_part(cn)
                    square(cn + 1)

            norm_group(0)
            square(0)
            for n in range(NS):
                prepare(n, 0, 0)

            def chunk(c, j):
                for n in range(NS):
                    decay(c, j, n)
                    copy_c(c, n)
                    prepare(n, c + 1, 1 - j)

            pairs(act, chunk)

        @block.vector
        def _(dve):
            v = nc.vector

            def subtract_mean(cn):
                dve.wait_ge(mean_ready, cn + 1)
                dve.wait_ge(xz_ready, 2 * MT * cn)
                for k in range(KT):
                    v.tensor_tensor(dn[:, k], xh[:, k], psp[:, 0], ALU.subtract).then_inc(d_ready, 1)

            def keep_tail(cn):
                dve.wait_ge(conv_ready, MT * cn)
                dve.wait_ge(conv_first, MT * cn)
                v.tensor_scalar(xi[:, :, 0:TAPS - 1], xi[:, :, T:T + TAPS - 1], keep[:, ds1(cn)], None,
                                ALU.mult).then_inc(tail_kept, 1)

            def conv(cn, ms):
                for k in range(1, TAPS):
                    for m in ms:
                        if k == 1:
                            dve.wait_ge(conv_first, MT * cn + m + 1)
                        else:
                            dve.wait_ge(conv_part, (TAPS - 2) * MT * cn + (TAPS - 2) * ms[0] + len(ms) * (k - 2) + (m - ms[0]) + 1)
                        v.scalar_tensor_tensor(out=cv[:, m], in0=xi[:, m, k:k + T], scalar=taps[:, m, k:k + 1],
                                               in1=cv[:, m], op0=ALU.mult, op1=ALU.add)\
                            .then_inc(conv_ready if k == TAPS - 1 else conv_part, 1)

            def split_bc(cn, jn):
                G = 2 * NS
                dve.wait_ge(bc_ready, cn + 1)
                v.tensor_copy(bcr[:], psp[0:G, 0]).then_inc(bc_part, 1)
                dve.wait_ge(bc_part, 5 * cn + 1)
                v.tensor_tensor(bcf[:, 0], psp[0:G, 0], bcr[:], ALU.subtract).then_inc(bc_part, 1)
                v.tensor_copy(bc3[jn][0:G], bcr[:]).then_inc(bc_part, 1)
                v.tensor_copy(dlow[:], psp[G:G + DTR, 0]).then_inc(dlow_copied, 1)
                dve.wait_ge(bc_part, 5 * cn + 3)
                v.tensor_copy(bcr[:], bcf[:, 0]).then_inc(bc_part, 1)
                dve.wait_ge(bc_part, 5 * cn + 4)
                v.tensor_tensor(bcf[:, 1], bcf[:, 0], bcr[:], ALU.subtract).then_inc(bc_part, 1)
                v.tensor_copy(bc3[jn][G:2 * G], bcr[:]).then_inc(bc_split, 1)
                dve.wait_ge(bc_part, 5 * cn + 5)
                v.tensor_copy(bc3[jn][2 * G:3 * G], bcf[:, 1]).then_inc(bc_split, 1)

            def dt_and_dtx(cn, jn):
                dve.wait_ge(u_copied, MT * (cn + 1))
                dve.wait_ge(sp_ready, 2 * cn + 2)
                v.scalar_tensor_tensor(out=dt[jn][:], in0=dt[jn][:], scalar=0.0, in1=cv[:], op0=ALU.max,
                                       op1=ALU.add).then_inc(dt_ready, 1)
                dve.wait_ge(dt_ready, cn + 1)
                dve.wait_ge(xc_ready, cn + 1)
                v.tensor_tensor(dtx[jn][:], dt[jn][:], xc[jn][:], ALU.mult).then_inc(dtx_ready, 1)

            def skip(c, jp):
                dve.wait_ge(slot_free, NS * c + SLOTS)
                for m in range(MT):
                    v.scalar_tensor_tensor(out=xc[jp][:, m], in0=xc[jp][:, m], scalar=d_skip[:, m:m + 1],
                                           in1=psy[:, m], op0=ALU.mult, op1=ALU.add).then_inc(y_skip, 1)

            def residual(c):
                dve.wait_ge(xr_loaded, 16 * (c + 1))
                for k in range(KT):
                    dve.wait_ge(out_ready, KT * c + k + 1)
                    v.tensor_tensor(xr[:, k], xr[:, k], psp[:, k], ALU.add).then_inc(x1_ready, 1)

            def scan_step(c, j, n):
                if n == 0:
                    dve.wait_ge(dtx_ready, c + 1)
                dve.wait_ge(b_ready, NS * c + n + 1)
                dve.wait_ge(slot_free, NS * c + n + 1)
                slot = st[:, n % SLOTS]
                v.tensor_tensor(slot, dtx[j][:], psb[:].unsqueeze(1).to_broadcast([P, MT, T]), ALU.mult)\
                    .then_inc(drive_ready, 1)
                dve.wait_ge(drive_ready, NS * c + n + 1)
                dve.wait_ge(last_kept, NS * c + n + 1)
                for m in range(MT):
                    dve.wait_ge(dec_ready, MT * (NS * c + n) + m + 1)
                    v.tensor_tensor_scan(slot[:, m], dec[:, n % 2, m], slot[:, m], last[:, n, m:m + 1],
                                         ALU.mult, ALU.add).then_inc(states_ready, 1)
                dve.wait_ge(states_ready, MT * (NS * c + n + 1 + 2))
                v.tensor_scalar(last[:, n].unsqueeze(2), slot[:, :, T - 1:T], keep[:, ds1(c + 1)], None,
                                ALU.mult).then_inc(last_kept, 1)

            v.memset(keep[:], 1.0).then_inc(set_up, 1)
            v.memset(epsc[:, 0:1], LN_EPS)
            v.memset(epsc[:, 1:2], 1.0).then_inc(set_up, 1)
            dve.wait_ge(set_up, 1)
            for b in range(B + 1):
                v.memset(keep[:, b * CPB:b * CPB + 1], 0.0)
            v.memset(xi[:], 0.0).then_inc(set_up, 1)
            v.memset(last[:], 0.0).then_inc(last_kept, NS)
            v.memset(psy[:], 0.0).then_inc(slot_free, SLOTS - LAG)
            v.memset(st[:], 0.0).then_inc(hc_ready, 2)
            v.memset(sz[1][:], 0.0).then_inc(states_ready, 2 * MT)
            v.memset(xc[1][:], 0.0)
            v.memset(cv[:], 0.0).then_inc(set_up, 1)
            dve.wait_ge(w_loaded, 16 * len(WLOADS))
            dve.wait_ge(set_up, 4)

            def prepare(n, cn, jn):
                if n == 2:
                    keep_tail(cn)
                if n == 7:
                    conv(cn, (0, 1))
                if n == 8:
                    conv(cn, (2, 3))
                if n == 11:
                    split_bc(cn, jn)
                if n == 15:
                    dt_and_dtx(cn, jn)

            def before_scan(n, cn, jn):
                if n == 15:
                    subtract_mean(cn + 1)

            subtract_mean(0)
            for n in range(NS):
                before_scan(n, 0, 0)
                prepare(n, 0, 0)

            def chunk(c, j):
                for n in range(NS):
                    if n == 2:
                        skip(c, 1 - j)
                    if n == 10:
                        residual(c)
                    before_scan(n, c + 1, 1 - j)
                    scan_step(c, j, n)
                    prepare(n, c + 1, 1 - j)

            pairs(dve, chunk)
            skip(NCH, 1)
            residual(NCH)

        @block.gpsimd
        def _(pool):
            g = nc.gpsimd

            def gate(c, jp):
                pool.wait_ge(y_skip, MT * (c + 1))
                pool.wait_ge(sz_ready, c)
                g.tensor_tensor(xc[jp][:], xc[jp][:], sz[jp][:], ALU.mult).then_inc(y_gated, 1)

            def times_rstd(cn):
                pool.wait_ge(rs_ready, cn + 1)
                pool.wait_ge(sq_ready, cn + 1)
                for k in range(KT):
                    g.tensor_tensor(dn[:, k], dn[:, k], rs[:], ALU.mult).then_inc(dn_ready, 1)

            times_rstd(0)

            def chunk(c, j):
                for n in range(NS):
                    if n == 2:
                        times_rstd(c + 1)
                    if n == 5:
                        gate(c, 1 - j)
                    pool.wait_ge(c_copied, NS * c + n + 1)
                    pool.wait_ge(last_kept, NS * c + n + 1 + NS)
                    g.tensor_tensor(st[:, n % SLOTS], st[:, n % SLOTS],
                                    cb[:, n % 2].unsqueeze(1).to_broadcast([P, MT, T]), ALU.mult).then_inc(hc_ready, 1)

            pairs(pool, chunk)
            gate(NCH, 1)

        @block.tensor
        def _(pe):
            t = nc.tensor
            G3 = 3 * 2 * NS

            def sum_channels(src, bank, signal):
                for k in range(KT):
                    ins = t.matmul(psp[:, bank], ones[:], src[:, k], start=(k == 0), stop=(k == KT - 1))
                ins.then_inc(signal, 1)

            def mean(cn):
                pe.wait_ge(xh_ready, KT * (cn + 1))
                pe.wait_ge(u_copied, MT * cn)
                sum_channels(xh, 0, mean_ready)

            def variance(cn):
                pe.wait_ge(sq_ready, cn + 1)
                sum_channels(sq, 1, var_ready)

            def in_product(cn, m):
                if m == 0:
                    pe.wait_ge(xn_ready, KT * (cn + 1))
                    pe.wait_ge(d_ready, KT * (cn + 1))
                elif m == 1:
                    pe.wait_ge(ln_ready, cn + 1)
                else:
                    pe.wait_ge(xz_copied, 2 * MT * cn + m - 1)
                for k in range(KT):
                    ins = t.matmul(psp[:, m % 2], w_in[:, k, m * P:(m + 1) * P], dn[:, k],
                                   start=(k == 0), stop=(k == KT - 1))
                ins.then_inc(xz_ready, 1)

            def x_products(cn, jn):
                pe.wait_ge(xc_ready, cn + 1)
                pe.wait_ge(xz_copied, 2 * MT * (cn + 1))
                pe.wait_ge(x1_ready, KT * cn)
                for m in range(MT):
                    ins = t.matmul(psp[0:2 * NS + DTR, 0], w_x[:, m], xc[jn][:, m], start=(m == 0), stop=(m == MT - 1))
                ins.then_inc(bc_ready, 1)

            def dt_product(cn, m):
                if m == 0:
                    pe.wait_ge(dlow_copied, cn + 1)
                    pe.wait_ge(bc_part, 5 * cn + 2)
                elif m >= 2:
                    pe.wait_ge(u_copied, MT * cn + m - 1)
                t.matmul(psp[:, m % 2], w_dt[:, m * P:(m + 1) * P], dlow[:], start=True, stop=True).then_inc(u_ready, 1)

            def out_product(c, jp, at_end=False):
                pe.wait_ge(y_gated, c + 1)
                if at_end:
                    pe.wait_ge(d_ready, KT * (c + 2))
                else:
                    pe.wait_ge(xz_copied, 2 * MT * (c + 2))
                for k in range(KT):
                    for m in range(MT):
                        ins = t.matmul(psp[:, k], w_out[:, m, k * P:(k + 1) * P], xc[jp][:, m],
                                       start=(m == 0), stop=(m == MT - 1))
                    ins.then_inc(out_ready, 1)

            def broadcast_b(c, j, n):
                if n == 0:
                    pe.wait_ge(bc_split, 2 * (c + 1))
                pe.wait_ge(drive_ready, NS * c + n)
                t.matmul(psb[:], select[:, n], bc3[j][:], start=True, stop=True).then_inc(b_ready, 1)

            def broadcast_c(c, j, n):
                pe.wait_ge(c_copied, NS * c + n)
                t.matmul(psc[:], select[:, NS + n], bc3[j][:], start=True, stop=True).then_inc(c_ready, 1)

            def sum_states(c, i):
                n = (i - LAG) % NS
                pe.wait_ge(hc_ready, NS * c + i + 1)
                if n == 0:
                    pe.wait_ge(y_skip, MT * (c + 1))
                for m in range(MT):
                    ins = t.matmul(psy[:, m], ident[:], st[:, n % SLOTS, m], start=(n == 0), stop=(n == NS - 1),
                                   skip_group_check=True)
                ins.then_inc(slot_free, 1)

            def prepare(n, cn, jn):
                if n == 1:
                    variance(cn)
                if n in XZ_PRODUCT:
                    in_product(cn, 2 * XZ_PRODUCT.index(n))
                    in_product(cn, 2 * XZ_PRODUCT.index(n) + 1)
                if n == 10:
                    x_products(cn, jn)
                if n == 12:
                    dt_product(cn, 0)
                    dt_product(cn, 1)
                if n == 13:
                    dt_product(cn, 2)
                    dt_product(cn, 3)
                if n == 14:
                    mean(cn + 1)

            pe.wait_ge(w_loaded, 16 * len(WLOADS))
            pe.wait_ge(set_up, 4)
            mean(0)
            for n in range(NS):
                prepare(n, 0, 0)
            broadcast_b(0, 0, 0)
            broadcast_c(0, 0, 0)

            def chunk(c, j):
                for n in range(NS):
                    if n not in (1, LAG):
                        sum_states(c, n)
                    if n + 1 < NS:
                        broadcast_b(c, j, n + 1)
                        broadcast_c(c, j, n + 1)
                    if n == 0:
                        sum_states(c, 1)
                    if n == LAG:
                        sum_states(c, n)
                    if n == 8:
                        out_product(c, 1 - j)
                    prepare(n, c + 1, 1 - j)
                broadcast_b(c + 1, 1 - j, 0)
                broadcast_c(c + 1, 1 - j, 0)

            pairs(pe, chunk)
            for i in range(LAG):
                sum_states(NCH, i)
            out_product(NCH, 1, at_end=True)




UNIT = 1024.0


def qkv_layer(nc, sems, ctx, x1, w, q_parts, k_parts, v_rows, v_chan, own_score, scale_col, own_bias):
    def sb(name, shape, dt=F32):
        return ctx.enter_context(nc.sbuf_tensor("qkv_" + name, shape, dt))

    def sem(name):
        return sems.enter_context(nc.semaphore("qkv_" + name))

    ones = sb("ones", [P, P])
    w_nat = sb("w_nat", [P, 2 * KT, C])
    w_t = sb("w_t", [P, KT, 3 * C])
    temp = sb("temp", [P, 1])
    epsc = sb("eps", [P, 1])
    wsq = sb("wsq", [P, C])
    norm2 = sb("norm2", [P, 2 * KT])
    pmax = sb("pmax", [P, 2])
    gmax = sb("gmax", [P, 2])
    nrm = sb("nrm", [P, 2])
    fac = sb("fac", [P, 12])
    fq, fk = fac[:, 0:1], fac[:, 1:2]
    xb = sb("xb", [P, 2, KT, T])
    dn = sb("dn", [P, 2, KT, T])
    sq = sb("sq", [P, KT, T])
    rs = sb("rs", [P, T])
    heads = sb("heads", [P, P])
    full = sb("full", [P, 2 * KT, T])
    own = sb("own", [P, 2, KT, T])
    prod = sb("prod", [P, KT, T])
    part1 = sb("part1", [P, 2, T], F16)
    part2 = sb("part2", [P, 2, T], F16)
    vt = sb("vt", [P, 2, T // P, H, 2 * HD])
    psm = ctx.enter_context(nc.psum_tensor("qkv_psm", [P, 2, T], F32))
    psq = ctx.enter_context(nc.psum_tensor("qkv_psq", [P, 2, T], F32))
    psv = ctx.enter_context(nc.psum_tensor("qkv_psv", [P, T // P, C], F32))
    pso = ctx.enter_context(nc.psum_tensor("qkv_pso", [P, 2, T], F32))

    w_loaded = sem("w_loaded")
    steps = sem("vector_steps")
    max_ready = sem("max_ready")
    nrm_ready = sem("nrm_ready")
    x_loaded = [sem(f"x_loaded{j}") for j in range(2)]
    mean_ready = sem("mean_ready")
    d_ready = sem("d_ready")
    sq_ready = sem("sq_ready")
    var_ready = sem("var_ready")
    rs_ready = sem("rs_ready")
    xn_ready = sem("xn_ready")
    qk_ready = sem("qk_ready")
    qk_scaled = sem("qk_scaled")
    part1_ready = sem("part1_ready")
    part2_ready = sem("part2_ready")
    qk_stored = [sem(f"qk_stored{j}") for j in range(2)]
    v_ready = sem("v_ready")
    v_copied = sem("v_copied")
    v_stored = [sem(f"v_stored{j}") for j in range(2)]
    prod_ready = sem("prod_ready")
    own_ready = sem("own_ready")
    own_copied = sem("own_copied")
    own_stored = sem("own_stored")
    WL = [(ones[:], w["ones"]), (w_nat[:], w["w_qk"]), (w_t[:], w["w_qkv_t"]), (temp[:], w["temp"]),
          (heads[:], w["heads"])]
    NQ = 2 * KT
    TT = T // P
    NORMED, ALL = 9, 22

    def pairs(eng, body):
        with eng.Fori(0, NCH // 2) as i:
            for j in range(2):
                body(i, i * 2 + j, j)

    with nc.Block() as block:
        @block.sync
        def _(sp):
            for dst, src in WL:
                sp.dma_start(dst, src).then_inc(w_loaded, 16)

            for j in range(2):
                sp.dma_start(xb[:, j], x1[j + 1]).then_inc(x_loaded[j], 16)

            def chunk(i, c, j):
                sp.wait_ge(d_ready, c + 1)
                sp.dma_start(xb[:, j], chunk_view(x1, (c + 2) % NCH + 1)).then_inc(x_loaded[j], 16)
                b, cc = c // CPB, c % CPB
                for g in range(NQ):
                    sp.wait_ge(part2_ready, NQ * c + g + 1)
                    dst = q_parts if g < KT else k_parts
                    for n, part in enumerate((part1, part2)):
                        for hh in range(2):
                            sp.dma_start(dst[ds1(b * HP + (g % KT) * 2 + hh), n, :, bass.ds(cc * T, T)].rearrange("o r t -> (o r) t"),
                                         part[hh * P // 2:(hh + 1) * P // 2, g % 2]).then_inc(qk_stored[g % 2], 16)
                sp.wait_ge(v_copied, TT * (c + 1))
                for hp in range(HP):
                    sp.dma_start(v_rows[ds1(b * HP + hp), :, bass.ds(cc * TT, TT)].rearrange("o p t r -> (o p) t r"),
                                 vt[:, j, :, 2 * hp:2 * hp + 2].rearrange("p t h d -> p t (h d)"))\
                        .then_inc(v_stored[j], 16)
                sp.wait_ge(own_copied, 2 * KT * (c + 1))
                sp.dma_start(chunk_view(own_score, c), own[:, 0]).then_inc(own_stored, 16)
                sp.dma_start(chunk_view(v_chan, c), own[:, 1]).then_inc(own_stored, 16)

            pairs(sp, chunk)
            for j in range(2):
                sp.wait_ge(x_loaded[j], 16 * (NCH // 2 + 1))
            sp.wait_ge(own_stored, 32 * NCH)
            for j in range(2):
                sp.wait_ge(qk_stored[j], 16 * 4 * NQ // 2 * NCH)
                sp.wait_ge(v_stored[j], 16 * HP * NCH // 2)

        @block.gpsimd
        def _(pool):
            pool.wait_ge(steps, NORMED)
            nc.gpsimd.partition_all_reduce(gmax[:], pmax[:], P, RMAX).then_inc(max_ready, 1)

        @block.scalar
        def _(act):
            s = nc.scalar
            act.wait_ge(max_ready, 1)
            s.activation(nrm[:], gmax[:], ACT.Ln).then_inc(nrm_ready, 1)
            act.wait_ge(nrm_ready, 1)
            s.activation(nrm[:], nrm[:], ACT.Exp, scale=0.5).then_inc(nrm_ready, 1)
            act.wait_ge(steps, ALL)

            def square(cn, jn):
                act.wait_ge(d_ready, cn + 1)
                act.wait_ge(var_ready, cn)
                s.activation(sq[:], dn[:, jn], ACT.Square).then_inc(sq_ready, 1)

            def rstd(cn):
                act.wait_ge(var_ready, cn + 1)
                act.wait_ge(xn_ready, cn)
                s.activation(rs[:], psm[:, 1], ACT.Ln, bias=epsc[:, 0:1]).then_inc(rs_ready, 1)
                act.wait_ge(rs_ready, 2 * cn + 1)
                s.activation(rs[:], rs[:], ACT.Exp, scale=-0.5).then_inc(rs_ready, 1)

            square(0, 0)
            rstd(0)

            def chunk(i, c, j):
                for g in range(NQ):
                    act.wait_ge(qk_ready, NQ * c + g + 1)
                    act.wait_ge(part2_ready, NQ * c)
                    act.wait_ge(prod_ready, c)
                    s.activation(full[:, g], psq[:, g % 2], ACT.Identity, scale=fq if g < KT else fk)\
                        .then_inc(qk_scaled, 1)
                square(c + 1, 1 - j)
                act.wait_ge(v_ready, c + 1)
                act.wait_ge(v_stored[j], 16 * HP * i)
                for t in range(TT):
                    s.activation(vt[:, j, t, :, 0:HD], psv[:, t, 0:C].rearrange("p (h d) -> p h d", h=H), ACT.Copy)\
                        .then_inc(v_copied, 1)
                rstd(c + 1)
                act.wait_ge(own_stored, 32 * c)
                for n in range(2 * KT):
                    act.wait_ge(own_ready, 2 * KT * c + n + 1)
                    s.activation(own[:, n // KT, n % KT], pso[:, n % 2], ACT.Copy).then_inc(own_copied, 1)

            pairs(act, chunk)

        @block.vector
        def _(dve):
            v = nc.vector
            done = [0]

            def step(ins):
                done[0] += 1
                ins.then_inc(steps, 1)
                dve.wait_ge(steps, done[0])

            step(v.memset(epsc[:], LN_EPS))
            step(v.memset(vt[:], 0.0))
            step(v.memset(vt[:, :, :, :, HD:HD + 1], 1.0))
            dve.wait_ge(w_loaded, 16 * len(WL))
            for r in range(2 * KT):
                step(v.tensor_tensor_reduce(wsq[:], w_nat[:, r], w_nat[:, r], 1.0, 0.0, ALU.mult, ALU.add,
                                            norm2[:, r:r + 1]))
            step(v.tensor_reduce(pmax[:], norm2[:].rearrange("p (a b) -> p a b", a=2), AX.X, ALU.max))
            step(v.tensor_scalar(pmax[:], pmax[:], 1e-30, None, ALU.max))
            assert done[0] == NORMED
            dve.wait_ge(nrm_ready, 2)
            step(v.tensor_scalar(nrm[:], nrm[:], C ** 0.5 / UNIT, None, ALU.mult))
            step(v.reciprocal(fac[:, 2:4], nrm[:]))
            step(v.tensor_scalar(fac[:, 4:5], temp[:], 0.0, None, ALU.is_ge))
            step(v.tensor_scalar(fac[:, 5:6], fac[:, 4:5], 2.0, -1.0, ALU.mult, ALU.add))
            step(v.tensor_tensor(fq, fac[:, 2:3], fac[:, 5:6], ALU.mult))
            step(v.tensor_copy(fk, fac[:, 3:4]))
            step(v.tensor_tensor(fac[:, 6:7], fac[:, 2:3], fac[:, 3:4], ALU.mult))
            step(v.tensor_tensor(fac[:, 7:8], temp[:], fac[:, 5:6], ALU.mult))
            step(v.tensor_tensor(fac[:, 8:9], fac[:, 6:7], fac[:, 7:8], ALU.mult))
            step(v.reciprocal(fac[:, 9:10], fac[:, 8:9]))
            step(v.tensor_scalar(scale_col, fac[:, 9:10], C ** -0.5, None, ALU.mult))
            step(v.reciprocal(fac[:, 10:11], temp[:]))
            step(v.tensor_scalar(own_bias, fac[:, 10:11], 1e9, None, ALU.mult))
            assert done[0] == ALL

            def subtract_mean(cn, jn, loads):
                dve.wait_ge(x_loaded[jn], 16 * loads)
                dve.wait_ge(mean_ready, cn + 1)
                v.tensor_tensor(dn[:, jn], xb[:, jn], psm[:, 0].unsqueeze(1).to_broadcast([P, KT, T]), ALU.subtract)\
                    .then_inc(d_ready, 1)

            def times_rstd(cn, jn):
                dve.wait_ge(rs_ready, 2 * cn + 2)
                dve.wait_ge(sq_ready, cn + 1)
                v.tensor_tensor(dn[:, jn], dn[:, jn], rs[:].unsqueeze(1).to_broadcast([P, KT, T]), ALU.mult)\
                    .then_inc(xn_ready, 1)

            subtract_mean(0, 0, 1)
            times_rstd(0, 0)

            def chunk(i, c, j):
                for g in range(NQ):
                    dve.wait_ge(qk_scaled, NQ * c + g + 1)
                    dve.wait_ge(qk_stored[g % 2], 64 * (NQ // 2 * c + g // 2))
                    v.tensor_copy(part1[:, g % 2], full[:, g]).then_inc(part1_ready, 1)
                    dve.wait_ge(part1_ready, NQ * c + g + 1)
                    v.tensor_tensor(part2[:, g % 2], full[:, g], part1[:, g % 2], ALU.subtract)\
                        .then_inc(part2_ready, 1)
                    if g == NQ - 2:
                        dve.wait_ge(own_ready, 2 * KT * c)
                        subtract_mean(c + 1, 1 - j, i + j + 1)
                dve.wait_ge(own_ready, 2 * KT * c)
                v.tensor_tensor(prod[:], full[:, 0:KT], full[:, KT:2 * KT], ALU.mult).then_inc(prod_ready, 1)
                times_rstd(c + 1, 1 - j)

            pairs(dve, chunk)

        @block.tensor
        def _(pe):
            t = nc.tensor

            def sum_channels(src, bank, signal):
                for k in range(KT):
                    ins = t.matmul(psm[:, bank], ones[:], src[:, k], start=(k == 0), stop=(k == KT - 1))
                ins.then_inc(signal, 1)

            pe.wait_ge(w_loaded, 16 * len(WL))

            def mean(cn, jn, loads):
                pe.wait_ge(x_loaded[jn], 16 * loads)
                pe.wait_ge(d_ready, cn)
                sum_channels(xb[:, jn], 0, mean_ready)

            def variance(cn):
                pe.wait_ge(sq_ready, cn + 1)
                pe.wait_ge(rs_ready, 2 * cn)
                sum_channels(sq, 1, var_ready)

            mean(0, 0, 1)
            variance(0)

            def chunk(i, c, j):
                pe.wait_ge(xn_ready, c + 1)
                for g in range(NQ):
                    pe.wait_ge(qk_scaled, NQ * c + max(g - 1, 0))
                    for k in range(KT):
                        ins = t.matmul(psq[:, g % 2], w_t[:, k, g * P:(g + 1) * P], dn[:, j, k],
                                       start=(k == 0), stop=(k == KT - 1))
                    ins.then_inc(qk_ready, 1)
                    if g == 1:
                        mean(c + 1, 1 - j, i + j + 1)
                pe.wait_ge(v_copied, TT * c)
                for s in range(TT):
                    for k in range(KT):
                        ins = t.matmul(psv[:, s, 0:C], dn[:, j, k, s * P:(s + 1) * P], w_t[:, k, 2 * C:3 * C],
                                       start=(k == 0), stop=(k == KT - 1))
                ins.then_inc(v_ready, 1)
                variance(c + 1)
                for n in range(2 * KT):
                    pe.wait_ge(own_copied, 2 * KT * c + max(n - 1, 0))
                    if n < KT:
                        pe.wait_ge(prod_ready, c + 1)
                        ins = t.matmul(pso[:, n % 2], heads[:], prod[:, n], start=True, stop=True)
                    else:
                        for k in range(KT):
                            ins = t.matmul(pso[:, n % 2], w_t[:, k, 2 * C + (n - KT) * P:2 * C + (n - KT + 1) * P],
                                           dn[:, j, k], start=(k == 0), stop=(k == KT - 1))
                    ins.then_inc(own_ready, 1)

            pairs(pe, chunk)


QR = 3 * HD + 3
NKT = L // P
SHIFT_UNIT = 1024.0
OWN_OUT = -3e38


def attention_layer(nc, sems, ctx, w, q_parts, k_parts, v_rows, scale_col, o_rows, sum_rows, shift_parts):
    def sb(name, shape, dt=F32):
        return ctx.enter_context(nc.sbuf_tensor("at_" + name, shape, dt))

    def sem(name):
        return sems.enter_context(nc.semaphore("at_" + name))

    G = B * HP
    QT = T // P
    PIECES = 4
    PK = NKT // PIECES
    KC = L // T
    EX = 4
    UNITS = KC * 2 * QT
    PER_SLOT, FIRST = 3, 2
    BANKS = 3
    SPLIT = 8

    ident = sb("ident", [P, P])
    identb = sb("identb", [P, P], BF16)
    identm = sb("identm", [P, P], BF16)
    k_main = sb("k_main", [QR, 2, L], F16)
    k_max = sb("k_max", [3 * HD, 2, L], F16)
    v_sb = sb("v", [P, NKT, 2 * 2 * HD])
    q_st = [sb(f"q{j}", [QR, 2, T], F16) for j in range(2)]
    mx = sb("mx", [P, KC, 2 * QT])
    mrow = sb("mrow", [P, 4, 2 * QT])
    mp16 = sb("mp16", [P, 2, 2 * QT], F16)
    mp = sb("mp", [P, 3, 2 * QT])
    mpt = sb("mpt", [3 * 2 * QT, P], F16)
    ex = sb("ex", [P, EX, 2, T])
    o_sb = sb("o_sb", [P, T])
    ps_s = ctx.enter_context(nc.psum_tensor("at_ps_s", [P, 2, 2, T], F32))
    ps_m = ctx.enter_context(nc.psum_tensor("at_ps_m", [P, BANKS, T], F32))
    ps_o = ctx.enter_context(nc.psum_tensor("at_ps_o", [P, T], F32))

    w_loaded = sem("w_loaded")
    set_up = sem("set_up")
    kmax_loaded = [sem(f"kmax_loaded{p}") for p in range(PIECES)]
    kmain_loaded = [sem(f"kmain_loaded{p}") for p in range(PIECES)]
    v_loaded = [sem(f"v_loaded{p}") for p in range(PIECES)]
    q_loaded = [sem(f"q_loaded{j}") for j in range(2)]
    shift_stored = sem("shift_stored")
    shift_loaded = [sem(f"shift_loaded{j}") for j in range(2)]
    max_scores = sem("max_scores")
    max_taken = sem("max_taken")
    split_steps = sem("split_steps")
    parts_turned = sem("parts_turned")
    parts_copied = sem("parts_copied")
    scores_ready = sem("scores_ready")
    ex_ready = sem("ex_ready")
    ex_used = sem("ex_used")
    o_copied = sem("o_copied")
    o_stored = sem("o_stored")

    def load_rows(eng, dst, parts, g, order, cols, signal):
        for n, part in enumerate(order):
            src = parts[ds1(g), part, :, cols].rearrange("o (s d) t -> (o d) s t", s=2)
            eng.dma_start(dst[n * HD:(n + 1) * HD], src).then_inc(signal, 16)

    with nc.Block() as block:
        @block.sync
        def _(sp):
            sp.dma_start(ident[:], w["ident"]).then_inc(w_loaded, 16)

            def cols(p):
                return slice(p * PK * P, (p + 1) * PK * P)

            def load_kmax(g, p):
                load_rows(sp, k_max[:, :, cols(p)], k_parts, g, (0, 1, 0), cols(p), kmax_loaded[p])

            def load_kmain_v(g, p):
                load_rows(sp, k_main[0:3 * HD, :, cols(p)], k_parts, g, (0, 1, 0), cols(p), kmain_loaded[p])
                sp.dma_start(v_sb[:, p * PK:(p + 1) * PK], v_rows[ds1(g), :, p * PK:(p + 1) * PK]
                             .rearrange("o p k r -> (o p) k r")).then_inc(v_loaded[p], 16)

            def load_q(g, c):
                load_rows(sp, q_st[c % 2][0:3 * HD], q_parts, g, (0, 0, 1), slice(c * T, (c + 1) * T), q_loaded[c % 2])

            def load_shift(count, g, c):
                sp.wait_ge(parts_copied, count)
                place = shift_parts[ds1(g // HP), c, :, ds1(g % HP)]
                for n in range(3):
                    sp.dma_start(place[:, n].rearrange("a b s (q t) -> (a b s q) t", q=QT),
                                 mpt[n * 2 * QT:(n + 1) * 2 * QT]).then_inc(shift_stored, 16)
                sp.wait_ge(shift_stored, 48 * count)
                sp.dma_start(q_st[c % 2][3 * HD:QR], place.rearrange("a n b s t -> n (a b s) t")).then_inc(shift_loaded[c % 2], 16)

            load_q(0, 0)
            for p in range(PIECES):
                load_kmax(0, p)
            for p in range(PIECES):
                load_kmain_v(0, p)
            load_shift(1, 0, 0)

            with sp.Fori(0, G) as g:
                for c in range(KC):
                    turn = g * KC + c
                    gn, cn = (g, c + 1) if c + 1 < KC else ((g + 1) % G, 0)
                    sp.wait_ge(ex_used, EX + NKT * turn)
                    load_q(gn, cn)
                    for p in range(PIECES):
                        if p == PIECES - 1:
                            load_shift(turn + 2, gn, cn)
                        if c == KC - 2:
                            sp.wait_ge(max_scores, UNITS * (turn + 1) + (p + 1) * UNITS // PIECES)
                            load_kmax((g + 1) % G, p)
                        if c == KC - 1:
                            sp.wait_ge(ex_used, EX + NKT * turn + (p + 1) * PK)
                            load_kmain_v((g + 1) % G, p)
            for p in range(PIECES):
                sp.wait_ge(kmax_loaded[p], 48 * (G + 1))
                sp.wait_ge(kmain_loaded[p], 48 * (G + 1))
                sp.wait_ge(v_loaded[p], 16 * (G + 1))
            sp.wait_ge(q_loaded[0], 48 * (G * KC // 2 + 1))
            sp.wait_ge(shift_loaded[0], 16 * (G * KC // 2 + 1))

        @block.gpsimd
        def _(pool):
            with pool.Fori(0, G) as g:
                for c in range(KC):
                    pool.wait_ge(o_copied, g * KC + c + 1)
                    for s in range(2):
                        row = s * P // 2
                        pool.dma_start(o_rows[ds1(g), s, :, c].rearrange("o d t -> (o d) t"), o_sb[row:row + HD])\
                            .then_inc(o_stored, 16)
                        pool.dma_start(sum_rows[ds1(g // HP), c, ds1(g % HP), s].rearrange("a b t -> (a b) t"),
                                       o_sb[row + HD:row + HD + 1]).then_inc(o_stored, 16)
            pool.wait_ge(o_stored, 64 * G * KC)

        @block.scalar
        def _(act):
            with act.Fori(0, G) as g:
                for c in range(KC):
                    for k in range(NKT):
                        n = g * (KC * NKT) + (c * NKT + k)
                        act.wait_ge(scores_ready, n + 1)
                        act.wait_ge(ex_used, n + 1)
                        nc.scalar.activation(ex[:, k % EX], ps_s[:, k % 2], ACT.Exp, scale=scale_col).then_inc(ex_ready, 1)

        @block.vector
        def _(dve):
            v = nc.vector

            def take_max(tp, u):
                dve.wait_ge(max_scores, UNITS * tp + u + 1)
                v.tensor_reduce(mx[:, u // (2 * QT), u % (2 * QT):u % (2 * QT) + 1], ps_m[:, u % BANKS], AX.X, ALU.max)\
                    .then_inc(max_taken, 1)

            def split_shift(tp):
                count = [0]

                def step(ins):
                    count[0] += 1
                    ins.then_inc(split_steps, 1)
                    dve.wait_ge(split_steps, SPLIT * tp + count[0])

                dve.wait_ge(max_taken, UNITS * (tp + 1))
                step(v.tensor_reduce(mrow[:, 0], mx[:].rearrange("p k u -> p u k"), AX.X, ALU.max))
                step(v.tensor_scalar(mrow[:, 1], mrow[:, 0], -1.0 / SHIFT_UNIT, None, ALU.mult))
                step(v.tensor_copy(mp16[:, 0], mrow[:, 1]))
                step(v.tensor_copy(mp[:, 0], mp16[:, 0]))
                step(v.tensor_tensor(mrow[:, 2], mrow[:, 1], mp[:, 0], ALU.subtract))
                step(v.tensor_copy(mp16[:, 1], mrow[:, 2]))
                step(v.tensor_copy(mp[:, 1], mp16[:, 1]))
                step(v.tensor_tensor(mp[:, 2], mrow[:, 2], mp[:, 1], ALU.subtract))
                assert count[0] == SPLIT
                dve.wait_ge(parts_turned, tp + 1)
                v.tensor_copy(mpt[:], ps_m[0:3 * 2 * QT, BANKS - 1, 0:P]).then_inc(parts_copied, 1)

            def copy_out(turn):
                dve.wait_ge(ex_used, EX + NKT * (turn + 1))
                dve.wait_ge(o_stored, 64 * turn)
                v.tensor_copy(o_sb[:], ps_o[:]).then_inc(o_copied, 1)

            for j in range(2):
                v.memset(q_st[j][3 * HD:QR], 0.0)
            v.memset(k_main[3 * HD:QR], SHIFT_UNIT).then_inc(set_up, 1)
            dve.wait_ge(w_loaded, 16)
            v.tensor_copy(identb[:], ident[:]).then_inc(set_up, 1)
            v.tensor_scalar(identm[:], ident[:], OWN_OUT, None, ALU.mult).then_inc(set_up, 1)
            v.memset(mx[:], 0.0).then_inc(ex_used, EX)
            dve.wait_ge(ex_used, EX)
            for u in range(UNITS):
                take_max(0, u)
            split_shift(0)
            with dve.Fori(0, G) as g:
                for c in range(KC):
                    turn = g * KC + c
                    for u in range(UNITS):
                        take_max(turn + 1, u)
                    split_shift(turn + 1)
                    copy_out(turn)

        @block.tensor
        def _(pe):
            t = nc.tensor

            def max_unit(tp, half, gen, c, u):
                kc, s, q = u // (2 * QT), (u // QT) % 2, u % QT
                if u == 0:
                    pe.wait_ge(q_loaded[c % 2], 48 * half)
                if u % (UNITS // PIECES) == 0:
                    pe.wait_ge(kmax_loaded[u // (UNITS // PIECES)], 48 * gen)
                if u >= BANKS:
                    pe.wait_ge(max_taken, UNITS * tp + u - BANKS + 1)
                elif u == BANKS - 1 and not isinstance(tp, int):
                    pe.wait_ge(parts_copied, tp)
                ins = t.matmul(ps_m[:, u % BANKS], q_st[c % 2][0:3 * HD, s, q * P:(q + 1) * P],
                               k_max[:, s, kc * T:(kc + 1) * T], start=True, stop=True)
                if kc == c:
                    ins = t.matmul(ps_m[:, u % BANKS, q * P:(q + 1) * P], identm[:], identb[:], start=False, stop=True,
                                   skip_group_check=True)
                ins.then_inc(max_scores, 1)

            def turn_parts(tp):
                pe.wait_ge(split_steps, SPLIT * (tp + 1))
                t.transpose(ps_m[0:3 * 2 * QT, BANKS - 1, 0:P], mp[:].rearrange("p n u -> p (n u)"), ident[:]).then_inc(parts_turned, 1)

            def scores(n, gen, half, c, k, s):
                if s == 0:
                    if k == 0:
                        pe.wait_ge(shift_loaded[c % 2], 16 * half)
                    if k % PK == 0:
                        pe.wait_ge(kmain_loaded[k // PK], 48 * gen)
                    if not isinstance(n, int):
                        pe.wait_ge(ex_ready, n - 1)
                d = k - c * QT
                ins = t.matmul(ps_s[:, k % 2, s], k_main[:, s, k * P:(k + 1) * P], q_st[c % 2][:, s],
                               start=True, stop=True)
                if 0 <= d < QT:
                    ins = t.matmul(ps_s[:, k % 2, s, d * P:(d + 1) * P], identm[:], identb[:], start=False, stop=True,
                                   skip_group_check=True)
                if s == 1:
                    ins.then_inc(scores_ready, 1)

            def values(turn, n, gen, k, s):
                if s == 0:
                    pe.wait_ge(ex_ready, n + 1)
                    if k == 0:
                        pe.wait_ge(o_copied, turn)
                    if k % PK == 0:
                        pe.wait_ge(v_loaded[k // PK], 16 * gen)
                ins = t.matmul(ps_o[s * P // 2:(s + 1) * P // 2], v_sb[:, k, s * 2 * HD:(s + 1) * 2 * HD],
                               ex[:, k % EX, s], start=(k == 0), stop=(k == NKT - 1), skip_group_check=True)
                if s == 1:
                    ins.then_inc(ex_used, 1)

            pe.wait_ge(w_loaded, 16)
            pe.wait_ge(set_up, 3)
            for u in range(UNITS):
                max_unit(0, 1, 1, 0, u)
            turn_parts(0)
            for s in range(2):
                scores(0, 1, 1, 0, 0, s)
            with pe.Fori(0, G) as g:
                for c in range(KC):
                    turn = g * KC + c
                    cn = (c + 1) % KC
                    gen_n = g + 1 if c + 1 < KC else g + 2
                    half_n = g * (KC // 2) + ((c + 1) // 2 + 1)
                    for k in range(NKT):
                        for s in range(2):
                            if k + 1 < NKT:
                                scores(turn * NKT + k + 1, g + 1, g * (KC // 2) + (c // 2 + 1), c, k + 1, s)
                            else:
                                scores(turn * NKT + NKT, gen_n, half_n, cn, 0, s)
                            u = (k - FIRST) * PER_SLOT + s
                            if u < UNITS and k >= FIRST:
                                max_unit(turn + 1, half_n, gen_n, cn, u)
                        if k == FIRST + UNITS // PER_SLOT + 3:
                            turn_parts(turn + 1)
                        for s in range(2):
                            values(turn, turn * NKT + k, g + 1, k, s)
                        u = (k - FIRST) * PER_SLOT + 2
                        if u < UNITS and k >= FIRST:
                            max_unit(turn + 1, half_n, gen_n, cn, u)




def expert_layer(nc, sems, ctx, x1, att, w, scale_col, own_bias, gates, out):
    def sb(name, shape, dt=F32):
        return ctx.enter_context(nc.sbuf_tensor("ex_" + name, shape, dt))

    def sem(name):
        return sems.enter_context(nc.semaphore("ex_" + name))

    TT = T // P
    ones = sb("ones", [P, P])
    ident = sb("ident", [P, P])
    w_p = sb("w_p", [P, KT, C])
    w_r = sb("w_r", [P, KT, E_])
    w1 = sb("w1", [P, E_, KT, C])
    w2 = sb("w2", [P, E_, KT, C])
    b2 = sb("b2", [E_, C])
    b1 = sb("b1", [P, E_, KT])
    b_p = sb("b_p", [P, KT])
    iota = sb("iota", [P, E_])
    epsc = sb("eps", [P, 1])
    xb = sb("xb", [P, KT, T])
    nb = sb("nb", [P, KT, T])
    vb = sb("vb", [P, KT, T])
    sb_ = sb("sb", [P, KT, T])
    dr = sb("dr", [H, T])
    mr = sb("mr", [3 * H, T], F16)
    lnd = sb("lnd", [P, KT, T])
    lse = sb("lse", [P, KT, T])
    den1 = sb("den1", [P, KT, T])
    spread = sb("spread", [H, C])
    spread3 = sb("spread3", [3 * H, C], F16)
    ob = [sb(f"ob{j}", [P, KT, T]) for j in range(2)]
    t2 = [sb(f"t2_{j}", [P, KT, T]) for j in range(2)]
    xn = [sb(f"xn{j}", [P, KT, T]) for j in range(2)]
    sq = sb("sq", [P, KT, T])
    rs = sb("rs", [P, T])
    lg = sb("lg", [P, TT, E_])
    top = sb("top", [P, TT, 8])
    idx = sb("idx", [P, TT, 8], U32)
    idf = sb("idf", [P, TT, 8])
    rw = sb("rw", [P, 4, TT])
    den = sb("den", [P, TT])
    mark = sb("mark", [P, 1])
    gt = sb("gt", [P, 3, TT, E_])
    gT = [sb(f"gT{j}", [E_, T]) for j in range(2)]
    gb = [sb(f"gb{j}", [P, E_, T]) for j in range(2)]
    hg = sb("hg", [P, 2, KT, T])
    yo = sb("yo", [P, KT, T])
    psy = ctx.enter_context(nc.psum_tensor("ex_psy", [P, KT, T], F32))
    psh = ctx.enter_context(nc.psum_tensor("ex_psh", [P, 2, KT, T], F32))
    psa = ctx.enter_context(nc.psum_tensor("ex_psa", [P, T], F32))
    psr = ctx.enter_context(nc.psum_tensor("ex_psr", [P, T], F32))

    w_loaded = sem("w_loaded")
    set_up = sem("set_up")
    x_loaded = sem("x_loaded")
    rows_loaded = sem("rows_loaded")
    score_loaded = sem("score_loaded")
    att_loaded = sem("att_loaded")
    sums_spread = sem("sums_spread")
    log_ready = sem("log_ready")
    shift_spread = sem("shift_spread")
    lse_ready = sem("lse_ready")
    own_ready = sem("own_ready")
    own_diff = sem("own_diff")
    own_exp = sem("own_exp")
    inv_ready = sem("inv_ready")
    share_steps = sem("share_steps")
    ob_ready = sem("ob_ready")
    sum_ready = sem("sum_ready")
    proj_ready = sem("proj_ready")
    t2_ready = sem("t2_ready")
    mean_ready = sem("mean_ready")
    d_ready = sem("d_ready")
    sq_ready = sem("sq_ready")
    var_ready = sem("var_ready")
    rs_ready = sem("rs_ready")
    xn_ready = sem("xn_ready")
    logits_ready = sem("logits_ready")
    gate_steps = sem("gate_steps")
    exp_ready = sem("exp_ready")
    gates_summed = sem("gates_summed")
    gates_turned = sem("gates_turned")
    gT_ready = sem("gT_ready")
    gates_stored = sem("gates_stored")
    gb_loaded = sem("gb_loaded")
    h_ready = sem("h_ready")
    gelu_ready = sem("gelu_ready")
    gated = sem("gated")
    y_ready = sem("y_ready")
    out_ready = sem("out_ready")
    out_stored = sem("out_stored")
    WL = [(ones[:], w["ones"]), (ident[:], w["ident"]), (w_p[:], w["w_p"]), (w_r[:], w["w_r"]), (w1[:], w["w1"]),
          (w2[:], w["w2"]), (b2[:], w["b2"]), (b1[:], w["b1"]), (b_p[:], w["b_p"]), (iota[:], w["iota"]),
          (spread[:], w["spread"]), (spread3[:], w["spread3"])]
    GS = 1 + 2 * TT + 3 + 2 + 2 * TT

    def pairs(eng, body):
        with eng.Fori(0, NCH // 2) as i:
            for j in range(2):
                body(i * 2 + j, j)

    with nc.Block() as block:
        @block.sync
        def _(sp):
            def load_x(slot):
                sp.dma_start(xb[:], chunk_view(x1, slot)).then_inc(x_loaded, 16)

            def load_attention(n, b, cc):
                sp.dma_start(dr[:], att["sum_rows"][ds1(b), ds1(cc)].rearrange("b c h s t -> (b c h s) t"))\
                    .then_inc(rows_loaded, 16)
                sp.dma_start(mr[:], att["shift_parts"][ds1(b), ds1(cc)].rearrange("b c n h s t -> (b c n h s) t"))\
                    .then_inc(rows_loaded, 16)
                sp.dma_start(sb_[:], chunk_view(att["own_score"], n)).then_inc(score_loaded, 16)
                sp.dma_start(nb[:], att["o_rows"][ds1(b), :, :, ds1(cc)].rearrange("b k p c t -> p (b k c) t"))\
                    .then_inc(att_loaded, 16)
                sp.dma_start(vb[:], chunk_view(att["v_chan"], n)).then_inc(att_loaded, 16)

            def spread_gates(cn, jn, first=False):
                stored = 16 if first else sp.snap(16 * (cn + 1))
                if not first:
                    sp.wait_ge(gated, E_ * (cn - 1))
                sp.wait_ge(gT_ready, cn + 1)
                sp.dma_start(gates, gT[jn][:]).then_inc(gates_stored, 16)
                sp.wait_ge(gates_stored, stored)
                sp.dma_start(gb[jn][:], gates.partition_broadcast(P)).then_inc(gb_loaded, 16)

            for dst, src in WL:
                sp.dma_start(dst, src).then_inc(w_loaded, 16)
            load_attention(0, 0, 0)
            load_x(1)
            sp.wait_ge(ob_ready, 1)
            load_attention(1, 0, 1)
            spread_gates(0, 0, first=True)

            def chunk(c, j):
                slot = sp.snap((c + 1) % NCH + 1)
                n = sp.snap((c + 2) % NCH)
                b, cc = sp.snap(n // CPB), sp.snap(n % CPB)
                sp.wait_ge(t2_ready, KT * (c + 1))
                load_x(slot)
                sp.wait_ge(ob_ready, c + 2)
                load_attention(n, b, cc)
                spread_gates(c + 1, 1 - j)
                sp.wait_ge(out_ready, c + 1)
                sp.dma_start(chunk_view(out, c), yo[:]).then_inc(out_stored, 16)

            pairs(sp, chunk)
            sp.wait_ge(out_stored, 16 * NCH)
            sp.wait_ge(gb_loaded, 16 * (NCH + 1))
            sp.wait_ge(x_loaded, 16 * (NCH + 1))
            sp.wait_ge(att_loaded, 32 * (NCH + 2))

        @block.scalar
        def _(act):
            s = nc.scalar

            def gelu(c, e):
                for m in range(KT):
                    act.wait_ge(h_ready, KT * (E_ * c + e) + m + 1)
                    act.wait_ge(y_ready, E_ * c + e + 1)
                    s.activation(hg[:, e % 2, m], psh[:, e % 2, m], ACT.Gelu, bias=b1[:, e, m:m + 1]).then_inc(gelu_ready, 1)

            def prepare(e, cn, jn):
                if e == 2:
                    act.wait_ge(d_ready, cn + 1)
                    act.wait_ge(var_ready, cn)
                    s.activation(sq[:], xn[jn][:], ACT.Square).then_inc(sq_ready, 1)
                if e == 4:
                    act.wait_ge(var_ready, cn + 1)
                    act.wait_ge(xn_ready, cn)
                    s.activation(rs[:], psa[:], ACT.Ln, bias=epsc[:, 0:1]).then_inc(rs_ready, 1)
                    act.wait_ge(rs_ready, 2 * cn + 1)
                    s.activation(rs[:], rs[:], ACT.Exp, scale=-0.5).then_inc(rs_ready, 1)
                if e == 5:
                    act.wait_ge(gate_steps, GS * cn + 1 + 2 * TT + 2)
                    s.activation(rw[:, 1], rw[:, 0], ACT.Exp).then_inc(exp_ready, 1)

            def combine(e, c2, j2):
                if e == 1:
                    act.wait_ge(ob_ready, c2)
                    for k in range(KT):
                        act.wait_ge(sums_spread, KT * c2 + k + 1)
                        s.activation(lnd[:, k], psr[:], ACT.Ln).then_inc(log_ready, 1)
                if e == 3:
                    act.wait_ge(own_ready, c2 + 1)
                    s.activation(sb_[:], sb_[:], ACT.Exp, scale=-1.0).then_inc(own_exp, 1)
                    s.activation(lnd[:], lnd[:], ACT.Exp, scale=-1.0).then_inc(inv_ready, 1)

            act.wait_ge(w_loaded, 16 * len(WL))
            act.wait_ge(set_up, 1)
            for e in range(E_):
                combine(e, 0, 0)
            for e in range(E_):
                prepare(e, 0, 0)
                combine(e, 1, 1)

            def chunk(c, j):
                for e in range(E_):
                    gelu(c, e)
                    prepare(e, c + 1, 1 - j)
                    combine(e, c + 2, j)

            pairs(act, chunk)

        @block.vector
        def _(dve):
            v = nc.vector

            def gate(c, j, e):
                if e == 0:
                    dve.wait_ge(gb_loaded, 16 * (c + 1))
                dve.wait_ge(gelu_ready, KT * (E_ * c + e + 1))
                v.tensor_tensor(hg[:, e % 2], hg[:, e % 2], gb[j][:, e].unsqueeze(1).to_broadcast([P, KT, T]), ALU.mult)\
                    .then_inc(gated, 1)

            def output(c, j):
                dve.wait_ge(y_ready, E_ * (c + 1) + 2)
                dve.wait_ge(out_stored, 16 * c)
                v.tensor_tensor(yo[:], t2[j][:], psy[:], ALU.add).then_inc(out_ready, 1)

            def gates_of(cn):
                count = [0]

                def step(ins, read=True):
                    count[0] += 1
                    ins.then_inc(gate_steps, 1)
                    if read:
                        dve.wait_ge(gate_steps, GS * cn + count[0])

                dve.wait_ge(logits_ready, cn + 1)
                step(v.tensor_copy(lg[:].rearrange("p t e -> p (t e)"), psr[:, 0:TT * E_]))
                v.memset(mark[:], 0.0)
                for tt in range(TT):
                    step(v.max(top[:, tt], lg[:, tt]), tt == TT - 1)
                v.memset(mark[:], 0.0)
                for tt in range(TT):
                    step(v.max_index(idx[:, tt], top[:, tt], lg[:, tt]), tt == TT - 1)
                step(v.tensor_copy(idf[:], idx[:]), False)
                step(v.tensor_tensor(rw[:, 0], top[:, :, 1], top[:, :, 0], ALU.subtract), False)
                dve.wait_ge(exp_ready, cn + 1)
                step(v.tensor_scalar(den[:], rw[:, 1], 1.0, None, ALU.add))
                step(v.reciprocal(rw[:, 2], den[:]))
                step(v.tensor_tensor(rw[:, 3], rw[:, 1], rw[:, 2], ALU.mult))
                for tt in range(TT):
                    for r in range(2):
                        step(v.tensor_scalar(gt[:, r, tt], iota[:], idf[:, tt, r:r + 1], rw[:, 2 + r, tt:tt + 1],
                                             ALU.is_equal, ALU.mult), r == 1 and tt == TT - 1)
                assert count[0] == GS
                v.tensor_tensor(gt[:, 2], gt[:, 0], gt[:, 1], ALU.add).then_inc(gates_summed, 1)

            def prepare(e, cn, jn):
                if e in (0, 1):
                    k = e
                    dve.wait_ge(proj_ready, KT * cn + k + 1)
                    dve.wait_ge(x_loaded, 16 * (cn + 1))
                    v.scalar_tensor_tensor(out=t2[jn][:, k], in0=psa[:], scalar=b_p[:, k:k + 1], in1=xb[:, k],
                                           op0=ALU.add, op1=ALU.add).then_inc(t2_ready, 1)
                if e == 2:
                    dve.wait_ge(mean_ready, cn + 1)
                    v.tensor_tensor(xn[jn][:], t2[jn][:], psa[:].unsqueeze(1).to_broadcast([P, KT, T]), ALU.subtract)\
                        .then_inc(d_ready, 1)
                if e == 4:
                    dve.wait_ge(rs_ready, 2 * cn + 2)
                    dve.wait_ge(sq_ready, cn + 1)
                    v.tensor_tensor(xn[jn][:], xn[jn][:], rs[:].unsqueeze(1).to_broadcast([P, KT, T]), ALU.mult)\
                        .then_inc(xn_ready, 1)
                    dve.wait_ge(xn_ready, cn + 1)
                    v.tensor_tensor(t2[jn][:], t2[jn][:], xn[jn][:], ALU.add).then_inc(sum_ready, 1)
                if e == 5:
                    gates_of(cn)
                if e == 6:
                    dve.wait_ge(gates_turned, cn + 1)
                    v.tensor_copy(gT[jn][:], psr[0:E_, :]).then_inc(gT_ready, 1)

            def combine(e, c2, j2):
                def step(ins):
                    count[0] += 1
                    ins.then_inc(share_steps, 1)
                    dve.wait_ge(share_steps, 6 * c2 + count[0])

                count = [{3: 0, 6: 2, 7: 3}.get(e, 0)]
                if e == 2:
                    dve.wait_ge(log_ready, KT * (c2 + 1))
                    dve.wait_ge(score_loaded, 16 * (c2 + 1))
                    for k in range(KT):
                        dve.wait_ge(shift_spread, KT * c2 + k + 1)
                        v.scalar_tensor_tensor(out=lse[:, k], in0=psr[:], scalar=scale_col, in1=lnd[:, k],
                                               op0=ALU.mult, op1=ALU.add).then_inc(lse_ready, 1)
                    dve.wait_ge(lse_ready, KT * (c2 + 1))
                    v.scalar_tensor_tensor(out=lse[:], in0=sb_[:], scalar=scale_col, in1=lse[:],
                                           op0=ALU.mult, op1=ALU.subtract).then_inc(own_diff, 1)
                    dve.wait_ge(own_diff, c2 + 1)
                    v.tensor_scalar(sb_[:], lse[:], own_bias, -80.0, ALU.add, ALU.max).then_inc(own_ready, 1)
                if e == 3:
                    dve.wait_ge(own_exp, c2 + 1)
                    step(v.tensor_scalar(den1[:], sb_[:], 1.0, None, ALU.add))
                    step(v.reciprocal(sb_[:, 0], den1[:, 0]))
                if e == 6:
                    step(v.reciprocal(sb_[:, 1], den1[:, 1]))
                if e == 7:
                    dve.wait_ge(inv_ready, c2 + 1)
                    dve.wait_ge(att_loaded, 32 * (c2 + 1))
                    step(v.tensor_tensor(nb[:], nb[:], lnd[:], ALU.mult))
                    step(v.tensor_tensor(vb[:], vb[:], nb[:], ALU.subtract))
                    step(v.tensor_tensor(vb[:], vb[:], sb_[:], ALU.mult))
                    v.tensor_tensor(ob[j2][:], vb[:], nb[:], ALU.add).then_inc(ob_ready, 1)

            v.memset(epsc[:], LN_EPS).then_inc(set_up, 1)
            v.memset(rs[:], 0.0).then_inc(y_ready, 2)
            dve.wait_ge(w_loaded, 16 * len(WL))
            dve.wait_ge(y_ready, 2)
            for e in range(E_):
                combine(e, 0, 0)
            for e in range(E_):
                prepare(e, 0, 0)
                combine(e, 1, 1)

            def chunk(c, j):
                for e in range(E_):
                    gate(c, j, e)
                    prepare(e, c + 1, 1 - j)
                    combine(e, c + 2, j)
                output(c, j)

            pairs(dve, chunk)

        @block.tensor
        def _(pe):
            t = nc.tensor

            def hidden(c, j, e):
                if e == 0:
                    pe.wait_ge(xn_ready, c + 1)
                for m in range(KT):
                    for k in range(KT):
                        ins = t.matmul(psh[:, e % 2, m], w1[:, e, k, m * P:(m + 1) * P], xn[j][:, k],
                                       start=(k == 0), stop=(k == KT - 1))
                    ins.then_inc(h_ready, 1)

            def outputs(c, j, e):
                if e == 0:
                    pe.wait_ge(out_ready, c)
                    pe.wait_ge(gT_ready, c + 1)
                    for m in range(KT):
                        t.matmul(psy[:, m], b2[:, m * P:(m + 1) * P], gT[j][:], start=True, stop=False)
                pe.wait_ge(gated, E_ * c + e + 1)
                for m in range(KT):
                    for k in range(KT):
                        ins = t.matmul(psy[:, m], w2[:, e, k, m * P:(m + 1) * P], hg[:, e % 2, k],
                                       start=False, stop=(e == E_ - 1 and k == KT - 1))
                ins.then_inc(y_ready, 1)

            def project(cn, jn, m):
                if m == 0:
                    pe.wait_ge(ob_ready, cn + 1)
                else:
                    pe.wait_ge(t2_ready, KT * cn + m)
                for k in range(KT):
                    ins = t.matmul(psa[:], w_p[:, k, m * P:(m + 1) * P], ob[jn][:, k], start=(k == 0), stop=(k == KT - 1))
                ins.then_inc(proj_ready, 1)

            def sum_channels(src, signal):
                for k in range(KT):
                    ins = t.matmul(psa[:], ones[:], src[:, k], start=(k == 0), stop=(k == KT - 1))
                ins.then_inc(signal, 1)

            def prepare(e, cn, jn):
                if e == 0:
                    project(cn, jn, 0)
                if e == 1:
                    project(cn, jn, 1)
                if e == 2:
                    pe.wait_ge(t2_ready, KT * (cn + 1))
                    sum_channels(t2[jn], mean_ready)
                if e == 3:
                    pe.wait_ge(sq_ready, cn + 1)
                    sum_channels(sq, var_ready)
                if e == 4:
                    pe.wait_ge(xn_ready, cn + 1)
                    pe.wait_ge(lse_ready, KT * (cn + 2))
                    for tt in range(TT):
                        for k in range(KT):
                            ins = t.matmul(psr[:, tt * E_:(tt + 1) * E_], xn[jn][:, k, tt * P:(tt + 1) * P], w_r[:, k],
                                           start=(k == 0), stop=(k == KT - 1))
                    ins.then_inc(logits_ready, 1)
                if e == 6:
                    pe.wait_ge(gates_summed, cn + 1)
                    for tt in range(TT):
                        ins = t.transpose(psr[0:E_, tt * P:(tt + 1) * P], gt[:, 2, tt], ident[:])
                    ins.then_inc(gates_turned, 1)

            def combine(e, c2):
                if e == 1:
                    pe.wait_ge(rows_loaded, 32 * (c2 + 1))
                    for k in range(KT):
                        if k:
                            pe.wait_ge(log_ready, KT * c2 + k)
                        elif not isinstance(c2, int):
                            pe.wait_ge(gT_ready, c2 - 1)
                        elif c2:
                            pe.wait_ge(lse_ready, KT * c2)
                        t.matmul(psr[:], spread[:, k * P:(k + 1) * P], dr[:], start=True, stop=True).then_inc(sums_spread, 1)
                if e == 2:
                    for k in range(KT):
                        if k:
                            pe.wait_ge(lse_ready, KT * c2 + k)
                        else:
                            pe.wait_ge(log_ready, KT * (c2 + 1))
                        t.matmul(psr[:], spread3[:, k * P:(k + 1) * P], mr[:], start=True, stop=True).then_inc(shift_spread, 1)

            pe.wait_ge(w_loaded, 16 * len(WL))
            for e in range(E_):
                combine(e, 0)
            for e in range(E_):
                prepare(e, 0, 0)
                combine(e, 1)
            hidden(0, 0, 0)

            def chunk(c, j):
                for e in range(E_):
                    if e + 1 < E_:
                        hidden(c, j, e + 1)
                    else:
                        hidden(c + 1, 1 - j, 0)
                    outputs(c, j, e)
                    prepare(e, c + 1, 1 - j)
                    combine(e, c + 2)

            pairs(pe, chunk)




def to_chunks(x):
    return np.ascontiguousarray(np.asarray(x).reshape(B, KT, P, CPB, T).transpose(0, 3, 2, 1, 4)).reshape(NCH, P, KT, T)


def rows_to_tiles(a):
    a = np.asarray(a)
    return np.ascontiguousarray(a.reshape(-1, P, a.shape[1]).transpose(1, 0, 2))


def column(a):
    return np.asarray(a).reshape(-1, P).T


def constants():
    ident = np.eye(P, dtype=np.float32)
    group = C // 32
    gn_mean = np.kron(np.eye(P // group), np.full((group, group), 1.0 / group)).astype(np.float32)
    ones = np.full((P, P), 1.0 / C, np.float32)
    select = np.zeros((3, 2 * NS, 2 * NS, P), np.float32)
    for r in range(2 * NS):
        select[:, r, r] = 1.0
    heads = np.kron(np.eye(P // HD), np.ones((HD, HD))).astype(np.float32)
    spread = np.kron(np.eye(H), np.ones((1, HD))).astype(np.float32)
    spread3 = np.tile(spread, (3, 1)) * -SHIFT_UNIT
    iota = np.tile(np.arange(E_, dtype=np.float32), (P, 1))
    return {"iota": iota, "ident": ident, "gn_mean": gn_mean, "ones": ones, "heads": heads, "spread": spread, "spread3": spread3,
            "select": select.reshape(3 * 2 * NS, 2 * NS, P)}


def arrays_of(i):
    cols = np.concatenate([column(i["L0_conv_ln_g"]), column(i["L0_conv_ln_b"]),
                           np.asarray(i["L0_conv_conv_w"]).reshape(MT, P, TAPS).transpose(1, 0, 2).reshape(P, MT * TAPS),
                           column(i["L0_conv_conv_b"]), column(i["L0_conv_b_dt"]), column(i["L0_conv_D_skip"])], axis=1)
    w_x = np.asarray(i["L0_conv_W_x"])
    return {
        "x": to_chunks(i["x"]),
        "W_in": rows_to_tiles(i["L0_conv_W_in"]),
        "W_x": rows_to_tiles(np.concatenate([w_x[:, DTR:], w_x[:, 0:DTR]], axis=1)),
        "W_dt": np.asarray(i["L0_conv_W_dt"]),
        "W_out": rows_to_tiles(i["L0_conv_W_out"]),
        "A_log": rows_to_tiles(i["L0_conv_A_log"]),
        "cols": np.ascontiguousarray(cols),
        "w_qk": rows_to_tiles(np.asarray(i["L1_attn_w_qkv"])[0:2 * C]),
        "w_qkv_t": rows_to_tiles(np.asarray(i["L1_attn_w_qkv"]).T),
        "w_p": rows_to_tiles(np.asarray(i["L1_attn_w_proj"]).T),
        "b_p": np.ascontiguousarray(column(i["L1_attn_b_proj"])),
        "w_r": rows_to_tiles(np.asarray(i["L1_ffn_router_w"]).T),
        "w1": np.ascontiguousarray(np.asarray(i["L1_ffn_w1"]).reshape(E_, KT, P, C).transpose(2, 0, 1, 3)),
        "w2": np.ascontiguousarray(np.asarray(i["L1_ffn_w2"]).reshape(E_, KT, P, C).transpose(2, 0, 1, 3)),
        "b1": np.ascontiguousarray(np.asarray(i["L1_ffn_b1"]).reshape(E_, KT, P).transpose(2, 0, 1)),
        "b2": np.asarray(i["L1_ffn_b2"]),
        "temp": np.repeat(np.asarray(i["L1_attn_temperature"]).reshape(1, 1), P, axis=0),
    } | constants()


INPUTS = ("x", "W_in", "W_x", "W_dt", "W_out", "A_log", "cols", "w_qk", "w_qkv_t", "w_p", "b_p", "w_r",
          "w1", "w2", "b1", "b2", "temp", "iota", "ident", "gn_mean", "ones", "heads", "spread", "spread3", "select")


def build(nc, w, out):
    def dram(name, shape, dt=F32):
        return nc.dram_tensor(name, shape, dt, kind="Internal").ap()

    x1 = dram("x1", (NCH + 1, P, KT, T))
    q_parts = dram("q_parts", (B * HP, 2, 2 * HD, L), F16)
    k_parts = dram("k_parts", (B * HP, 2, 2 * HD, L), F16)
    v_rows = dram("v_rows", (B * HP, P, L // P, 4 * HD))
    att = {"v_chan": dram("v_chan", (NCH, P, KT, T)),
           "own_score": dram("own_score", (NCH, P, KT, T)),
           "o_rows": dram("o_rows", (B, KT, P, CPB, T)),
           "sum_rows": dram("sum_rows", (B, CPB, HP, 2, T)),
           "shift_parts": dram("shift_parts", (B, CPB, 3, HP, 2, T), F16)}
    gates = dram("gates", (E_, T))
    o_pairs = att["o_rows"].rearrange("b k (x s d) c t -> (b k x) s d c t", x=2, s=2)

    with ExitStack() as sems:
        with ExitStack() as ctx:
            scale_of = ctx.enter_context(nc.sbuf_tensor("scale_of", [P, NCH, KT], F32))
            shift_of = ctx.enter_context(nc.sbuf_tensor("shift_of", [P, NCH, KT], F32))
            with ExitStack() as part:
                group_norm_stats(nc, sems, part, w["x"], w["gn_mean"], scale_of, shift_of)
            with ExitStack() as part:
                state_space_layer(nc, sems, part, w["x"], w, scale_of, shift_of, x1)
        with ExitStack() as ctx:
            score_scale = ctx.enter_context(nc.sbuf_tensor("score_scale", [P, 1], F32))
            own_bias = ctx.enter_context(nc.sbuf_tensor("own_bias", [P, 1], F32))
            with ExitStack() as part:
                qkv_layer(nc, sems, part, x1, w, q_parts, k_parts, v_rows, att["v_chan"], att["own_score"],
                          score_scale[:], own_bias[:, 0:1])
            with ExitStack() as part:
                attention_layer(nc, sems, part, w, q_parts, k_parts, v_rows, score_scale[:, 0:1], o_pairs,
                                att["sum_rows"], att["shift_parts"])
            with ExitStack() as part:
                expert_layer(nc, sems, part, x1, att, w, score_scale[:, 0:1], own_bias[:, 0:1], gates, out)


def kernel(**inputs):
    import ml_dtypes
    import concourse.bacc as bacc
    from concourse.bass_utils import run_bass_kernel_spmd

    arrays = arrays_of(inputs)
    arrays["select"] = arrays["select"].astype(ml_dtypes.bfloat16)
    arrays["spread3"] = arrays["spread3"].astype(np.float16)
    nc = bacc.Bacc("TRN2", target_bir_lowering=False, num_devices=1)
    feed, w = {}, {}
    for name in INPUTS:
        a = np.ascontiguousarray(arrays[name])
        feed[f"in_{name}"] = a
        w[name] = nc.dram_tensor(f"in_{name}", a.shape, mybir.dt.from_np(a.dtype), kind="ExternalInput").ap()
    out = nc.dram_tensor("out_chunks", (NCH, P, KT, T), F32, kind="ExternalOutput").ap()
    build(nc, w, out)
    r = run_bass_kernel_spmd(nc, [feed], core_ids=[0])
    y = np.asarray(r.results[0]["out_chunks"]).reshape(B, CPB, P, KT, T)
    return np.ascontiguousarray(y.transpose(0, 3, 2, 1, 4)).reshape(B, C, 64, 64)
```
